# Optimizing a Trainium2 kernel written in Bass

```python
import numpy as np
import jax
import jax.numpy as jnp

def _softmax(x, axis=-1):
    return jax.nn.softmax(x, axis=axis)

def _gelu(x):
    return jax.nn.gelu(x, approximate=True)

def _silu(x):
    return jax.nn.silu(x)

def _sigmoid(x):
    return jax.nn.sigmoid(x)

def _layernorm(x, axis=-1, eps=1e-05):
    m = jnp.mean(x, axis=axis, keepdims=True)
    v = jnp.var(x, axis=axis, keepdims=True)
    return (x - m) / jnp.sqrt(v + eps)

def _scatter_add(tgt, idx, src, axis=0):
    return tgt.at[idx].add(src)

def _segment_sum(src, seg, n):
    return jax.ops.segment_sum(src, seg, n)
kernel_name = 'mk_decoder_postln_d1_seqx_r8_5964ca'

def setup_inputs(seed: int=0):
    np.random.seed(seed)
    _w = jnp.asarray

    def _rec_inputs():
        import jax
        import jax.numpy as jnp
        _rk = jax.random.key(seed)
        x = -0.0005207 + 1.001 * jax.random.normal(jax.random.fold_in(_rk, 1), (4, 256, 512), jnp.float32)
        _lenS = 256 - jax.random.randint(jax.random.fold_in(_rk, 7), (4,), 0, max(1, 256 // 4) + 1, jnp.int32)
        _lenS2 = 1601 - jax.random.randint(jax.random.fold_in(_rk, 8), (4,), 0, max(1, 1601 // 4) + 1, jnp.int32)
        _ctx_4096P = jax.random.normal(jax.random.fold_in(_rk, 11), (4, 16, 512), jnp.float32)
        _ctx_4096c = jax.random.dirichlet(jax.random.fold_in(_rk, 511), 0.3 * jnp.ones((16,), jnp.float32), (4, 1601))
        _ctx_4096t = jnp.einsum('bsk,bkd->bsd', _ctx_4096c, _ctx_4096P)
        _ctx_4096t = _ctx_4096t * jax.lax.rsqrt(jnp.mean(jnp.square(_ctx_4096t)) + 1e-12) * 0.953939
        ctx_4096 = -0.00010331 + 0.999899 * (_ctx_4096t + 0.3 * jax.random.normal(jax.random.fold_in(_rk, 611), (4, 1601, 512), jnp.float32))
        return (x, ctx_4096)
    x, ctx_4096 = _rec_inputs()

    def _L0_attn_setup():
        import jax, jax.numpy as jnp
        import numpy as np
        EMB = 512
        HEADS = 32
        SCALE = 4
        D = EMB // HEADS
        HKV = HEADS // SCALE
        B, S = (2, 256)
        key = jax.random.key(seed)
        ks = jax.random.split(key, 7)
        std = 0.02
        return {'x': jax.random.normal(ks[0], (B, S, EMB), jnp.float32), 'Wq': jax.random.normal(ks[1], (EMB, D, HEADS), jnp.float32) * std, 'bq': jnp.zeros((D, HEADS), jnp.float32), 'Wk': jax.random.normal(ks[2], (EMB, D, HKV), jnp.float32) * std, 'bk': jnp.zeros((D, HKV), jnp.float32), 'Wv': jax.random.normal(ks[3], (EMB, D, HKV), jnp.float32) * std, 'bv': jnp.zeros((D, HKV), jnp.float32)}
    _L0_attn_all = _L0_attn_setup()
    _L0_attn_in = {k: v for k, v in _L0_attn_all.items() if k in ('Wq', 'bq', 'Wk', 'bk', 'Wv', 'bv')}
    del _L0_attn_all

    def _L0_xattn_setup():
        import jax, jax.numpy as jnp
        import numpy as np
        HEADS = 32
        KV_HEADS = 8
        HEAD_DIM = 128
        EPS = 1e-06

        def rms_norm(x, w):
            var = jnp.mean(jnp.square(x.astype(jnp.float32)), axis=-1, keepdims=True)
            return (x.astype(jnp.float32) * jax.lax.rsqrt(var + EPS)).astype(x.dtype) * w
        key = jax.random.key(seed)
        ks = jax.random.split(key, 6)
        bsz, n_lat, seq, hidden = (8, 64, 512, 512)
        return {'latents': jax.random.normal(ks[0], (bsz, n_lat, hidden), jnp.float32), 'context': jax.random.normal(ks[1], (bsz, seq, hidden), jnp.float32), 'Wq': jax.random.normal(ks[2], (hidden, HEADS * HEAD_DIM), jnp.float32) * 0.02, 'Wk': jax.random.normal(ks[3], (hidden, KV_HEADS * HEAD_DIM), jnp.float32) * 0.02, 'Wv': jax.random.normal(ks[4], (hidden, KV_HEADS * HEAD_DIM), jnp.float32) * 0.02, 'Wo': jax.random.normal(ks[5], (HEADS * HEAD_DIM, hidden), jnp.float32) * 0.02, 'q_norm_w': jnp.ones((HEAD_DIM,), jnp.float32), 'k_norm_w': jnp.ones((HEAD_DIM,), jnp.float32)}
    _L0_xattn_all = _L0_xattn_setup()
    _L0_xattn_in = {k: v for k, v in _L0_xattn_all.items() if k in ('Wq', 'Wk', 'Wv', 'Wo', 'q_norm_w', 'k_norm_w')}
    del _L0_xattn_all

    def _L0_ffn_setup():
        import jax, jax.numpy as jnp
        import numpy as np
        K_TOP = 8
        key = jax.random.key(seed)
        k1, k2, k3 = jax.random.split(key, 3)
        B, S, H, E = (4, 512, 512, 64)
        hidden_states = jax.random.normal(k1, (B, S, H), dtype=jnp.float32)
        router_weight = jax.random.normal(k2, (E, H), dtype=jnp.float32)
        router_bias = jnp.zeros((E,), dtype=jnp.float32)
        expert_bias = jax.random.normal(k3, (E, H), dtype=jnp.float32) * 0.1
        return {'hidden_states': hidden_states, 'router_weight': router_weight, 'router_bias': router_bias, 'expert_bias': expert_bias}
    _L0_ffn_all = _L0_ffn_setup()
    _L0_ffn_in = {k: v for k, v in _L0_ffn_all.items() if k in ('router_weight', 'router_bias', 'expert_bias')}
    del _L0_ffn_all
    return {'x': x, 'ctx_4096': ctx_4096, 'L0_attn_Wq': _L0_attn_in['Wq'], 'L0_attn_bq': _L0_attn_in['bq'], 'L0_attn_Wk': _L0_attn_in['Wk'], 'L0_attn_bk': _L0_attn_in['bk'], 'L0_attn_Wv': _L0_attn_in['Wv'], 'L0_attn_bv': _L0_attn_in['bv'], 'L0_xattn_Wq': _L0_xattn_in['Wq'], 'L0_xattn_Wk': _L0_xattn_in['Wk'], 'L0_xattn_Wv': _L0_xattn_in['Wv'], 'L0_xattn_Wo': _L0_xattn_in['Wo'], 'L0_xattn_q_norm_w': _L0_xattn_in['q_norm_w'], 'L0_xattn_k_norm_w': _L0_xattn_in['k_norm_w'], 'L0_ffn_router_weight': _L0_ffn_in['router_weight'], 'L0_ffn_router_bias': _L0_ffn_in['router_bias'], 'L0_ffn_expert_bias': _L0_ffn_in['expert_bias']}

def reference(x, ctx_4096, L0_attn_Wq, L0_attn_bq, L0_attn_Wk, L0_attn_bk, L0_attn_Wv, L0_attn_bv, L0_xattn_Wq, L0_xattn_Wk, L0_xattn_Wv, L0_xattn_Wo, L0_xattn_q_norm_w, L0_xattn_k_norm_w, L0_ffn_router_weight, L0_ffn_router_bias, L0_ffn_expert_bias):
    import jax
    import jax.numpy as jnp

    def _L0_attn_ref(x, Wq, bq, Wk, bk, Wv, bv):
        import jax, jax.numpy as jnp
        import numpy as np
        EMB = 512
        HEADS = 32
        SCALE = 4
        D = EMB // HEADS
        HKV = HEADS // SCALE
        B, S = (2, 256)
        q = jnp.einsum('bse,edh->bsdh', x, Wq) + bq
        k = jnp.einsum('bse,edh->bsdh', x, Wk) + bk
        v = jnp.einsum('bse,edh->bsdh', x, Wv) + bv
        k = jnp.repeat(k, SCALE, axis=-1)
        v = jnp.repeat(v, SCALE, axis=-1)
        scores = jnp.einsum('bsdh,bseh->bsde', q, k) / np.float32(np.sqrt(D))
        attn = jax.nn.softmax(scores, axis=-1)
        out = jnp.einsum('bsde,bseh->bsdh', attn, v)
        return out.reshape(x.shape[:-1] + (EMB,))

    def _L0_xattn_ref(latents, context, Wq, Wk, Wv, Wo, q_norm_w, k_norm_w):
        import jax, jax.numpy as jnp
        import numpy as np
        HEADS = 32
        KV_HEADS = 8
        HEAD_DIM = 128
        EPS = 1e-06

        def rms_norm(x, w):
            var = jnp.mean(jnp.square(x.astype(jnp.float32)), axis=-1, keepdims=True)
            return (x.astype(jnp.float32) * jax.lax.rsqrt(var + EPS)).astype(x.dtype) * w
        bsz, q_len, hidden = latents.shape
        kv = jnp.concatenate([context, latents], axis=1)
        kv_len = kv.shape[1]
        groups = HEADS // KV_HEADS
        q = (latents @ Wq).reshape(bsz, q_len, HEADS, HEAD_DIM).transpose(0, 2, 1, 3)
        k = (kv @ Wk).reshape(bsz, kv_len, KV_HEADS, HEAD_DIM).transpose(0, 2, 1, 3)
        v = (kv @ Wv).reshape(bsz, kv_len, KV_HEADS, HEAD_DIM).transpose(0, 2, 1, 3)
        q = rms_norm(q, q_norm_w)
        k = rms_norm(k, k_norm_w)
        qg = q.reshape(bsz, KV_HEADS, groups, q_len, HEAD_DIM)
        scale = 1.0 / np.sqrt(HEAD_DIM)
        scores = jnp.einsum('bhgqd,bhkd->bhgqk', qg, k) * scale
        probs = jax.nn.softmax(scores.astype(jnp.float32), axis=-1).astype(q.dtype)
        out = jnp.einsum('bhgqk,bhkd->bhgqd', probs, v)
        out = out.reshape(bsz, HEADS, q_len, HEAD_DIM).transpose(0, 2, 1, 3)
        out = out.reshape(bsz, q_len, HEADS * HEAD_DIM)
        return out @ Wo

    def _L0_ffn_ref(hidden_states, router_weight, router_bias, expert_bias):
        import jax, jax.numpy as jnp
        import numpy as np
        K_TOP = 8
        B, S, H = hidden_states.shape
        E = router_weight.shape[0]
        T = B * S
        flat = hidden_states.reshape(T, H)
        logits = jnp.einsum('th,eh->te', flat, router_weight) + router_bias
        scores = jax.nn.softmax(logits, axis=-1)
        topk_w, topk_idx = jax.lax.top_k(scores, K_TOP)
        w_sum = topk_w.sum(axis=-1, keepdims=True)
        w_dense = jnp.zeros((T, E), dtype=scores.dtype).at[jnp.arange(T)[:, None], topk_idx].add(topk_w)
        bias_mix = jnp.einsum('te,eh->th', w_dense, expert_bias)
        out = flat * w_sum + bias_mix
        return out.reshape(B, S, H)
    x = _layernorm(x + _L0_attn_ref(x, L0_attn_Wq, L0_attn_bq, L0_attn_Wk, L0_attn_bk, L0_attn_Wv, L0_attn_bv), axis=-1)
    x = _layernorm(x + _L0_xattn_ref(x, ctx_4096, L0_xattn_Wq, L0_xattn_Wk, L0_xattn_Wv, L0_xattn_Wo, L0_xattn_q_norm_w, L0_xattn_k_norm_w), axis=-1)
    x = _layernorm(x + _L0_ffn_ref(x, L0_ffn_router_weight, L0_ffn_router_bias, L0_ffn_expert_bias), axis=-1)
    return x

_drawn_inputs = setup_inputs


def setup_inputs(seed=0):
    import zlib

    import numpy as np

    out = dict(_drawn_inputs(seed))
    spreads = {'L0_attn_bq': (0.0, 0.8),
     'L0_attn_bk': (0.0, 0.8),
     'L0_attn_bv': (0.0, 0.373),
     'L0_xattn_q_norm_w': (1.0, 0.6),
     'L0_xattn_k_norm_w': (1.0, 0.6),
     'L0_ffn_router_bias': (0.0, 0.8)}
    factors = {}
    for name, (base, spread) in spreads.items():
        noise = np.random.default_rng([zlib.crc32(name.encode()), seed]).standard_normal(out[name].shape)
        drawn = base * np.exp(spread * noise) if base else spread * noise
        out[name] = jnp.asarray(drawn.astype(out[name].dtype))
    for name, factor in factors.items():
        out[name] = (out[name] * factor).astype(out[name].dtype)
    return out
```

```python
from contextlib import ExitStack

import concourse.bass as bass
from concourse import mybir

F32 = mybir.dt.float32
F32R = mybir.dt.float32r
ALU = mybir.AluOpType
ACT = mybir.ActivationFunctionType
AX = mybir.AxisListType
P = 128


def f(ap):
    return ap.bitcast(F32)


def newton_rsqrt(e, nc, x, y0, a, out, step):
    sem, n = step
    e.scalar_tensor_tensor(a, x, -0.5, y0, ALU.mult, ALU.mult).then_inc(sem, 1)
    e.wait_ge(sem, n + 1)
    e.tensor_tensor(a, a, y0, ALU.mult).then_inc(sem, 1)
    e.wait_ge(sem, n + 2)
    return e.scalar_tensor_tensor(out, a, 1.5, y0, ALU.add, ALU.mult)


def self_attention(nc, x, Wq, bq, Wk, bk, Wv, bv, x1):
    B, S, E = x.shape
    D, H = Wq.shape[1:]
    G = Wk.shape[2]
    R = H // G
    C = E // P
    DG = D * G
    TPB = S // P

    with ExitStack() as ctx:
        def sb(name, shape, dt=F32):
            return ctx.enter_context(nc.sbuf_tensor(name, shape, dt))

        def sem(name):
            return ctx.enter_context(nc.semaphore(name))

        w_raw = sb("a_w_raw", [P, C, E])
        w = sb("a_w", [P, C, 3 * DG])
        b_raw = sb("a_b_raw", [1, E])
        bias = sb("a_bias", [1, 3 * DG])
        ones = sb("a_ones", [1, P])
        ident = sb("a_ident", [P, P])
        xt = sb("a_x", [P, TPB, E])
        xT = sb("a_xT", [P, TPB, C, P])
        qkv = sb("a_qkv", [P, TPB, 3 * DG])
        prod = sb("a_prod", [P, TPB, D * D * G])
        sc = sb("a_scores", [P, TPB, D, D])
        stat = sb("a_stat", [P, TPB, 3, D])
        o = sb("a_o", [P, TPB, DG])
        bn = sb("a_bn", [P, TPB, 6])
        mv = sb("a_mv", [P, TPB, 2])
        rs = sb("a_rs", [P, TPB, 5])
        tr = [ctx.enter_context(nc.psum_tensor(f"a_tr{i}", [P, C, P], F32)) for i in range(TPB)]
        pq = [ctx.enter_context(nc.psum_tensor(f"a_pq{i}", [P, 512], F32)) for i in range(TPB)]

        s_w = sem("a_w_loaded")
        s_wr = sem("a_w_reduced")
        s_cst = sem("a_constants")
        s_x = [sem(f"a_x_loaded{i}") for i in range(TPB)]
        s_tr = sem("a_transposed")
        s_xT = sem("a_xT_copied")
        s_pq = sem("a_projected")
        s_qkv = sem("a_qkv_copied")
        s_p1 = sem("a_qk_products")
        s_sc = sem("a_scores_summed")
        s_mx = sem("a_row_max")
        s_sh = sem("a_scores_shifted")
        s_ex = sem("a_exponentials")
        s_su = sem("a_row_sums")
        s_ri = sem("a_row_reciprocals")
        s_pr = sem("a_probabilities")
        s_p2 = sem("a_pv_products")
        s_o = sem("a_outputs_summed")
        s_h = sem("a_residual_added")
        s_bn = sem("a_bn_steps")
        s_go = sem("a_statistics_seen")
        s_va = sem("a_variance")
        s_ln = sem("a_log_variance")
        s_y0 = sem("a_rsqrt_estimate")
        s_nw = sem("a_newton_steps")
        s_x1 = sem("a_normalised")
        s_st = [sem(f"a_x1_stored{i}") for i in range(TPB)]

        block = ctx.enter_context(nc.Block())

        @block.sync
        def _(e):
            e.dma_start(w_raw[:], Wq.rearrange("(c p) d h -> p c (d h)", p=P)).then_inc(s_w, 16)
            e.dma_start(w[:, :, DG:2 * DG], Wk.rearrange("(c p) d g -> p c (d g)", p=P)).then_inc(s_w, 16)
            e.dma_start(w[:, :, 2 * DG:], Wv.rearrange("(c p) d g -> p c (d g)", p=P)).then_inc(s_w, 16)
            e.dma_start(b_raw[:], bq.rearrange("(o d) h -> o (d h)", o=1)).then_inc(s_w, 16)
            e.dma_start(bias[:, DG:2 * DG], bk.rearrange("(o d) g -> o (d g)", o=1)).then_inc(s_w, 16)
            e.dma_start(bias[:, 2 * DG:], bv.rearrange("(o d) g -> o (d g)", o=1)).then_inc(s_w, 16)
            with e.Fori(0, B) as b:
                for t in range(TPB):
                    e.wait_ge(s_st[t], 16 * b + 16)
                    e.dma_start(xt[:, t, :], x[bass.ds(b, 1), t * P:(t + 1) * P, :]
                                .rearrange("o p e -> (o p) e")).then_inc(s_x[t], 16)
                for t in range(TPB):
                    e.wait_ge(s_x1, TPB * b + t + 1)
                    e.dma_start(x1[bass.ds(b, 1), t * P:(t + 1) * P, :]
                                .rearrange("o p e -> (o p) e"), xt[:, t, :]).then_inc(s_st[t], 16)
            for t in range(TPB):
                e.wait_ge(s_st[t], 16 * B + 16)

        @block.gpsimd
        def _(e):
            for t in range(TPB):
                e.sem_inc(s_st[t], 16)
            e.memset(ones[:], 1.0).then_inc(s_cst, 1)
            e.memset(ident[:], 0.0).then_inc(s_cst, 1)
            e.wait_ge(s_cst, 2)
            e.affine_select(out=ident[:], in_=ident[:], compare_op=ALU.not_equal, fill=1.0, base=0,
                            pattern=[[-1, P]], channel_multiplier=1).then_inc(s_cst, 1)
            with e.Fori(0, B) as b:
                for t in range(TPB):
                    e.wait_ge(s_qkv, TPB * b + t + 1)
                    q = qkv[:, t, 0:DG].rearrange("p (d g) -> p d g", g=G)
                    k = qkv[:, t, DG:2 * DG].rearrange("p (e g) -> p e g", g=G)
                    e.tensor_tensor(prod[:, t, :].rearrange("p (d e g) -> p d e g", d=D, e=D),
                                    q.unsqueeze(2).to_broadcast([P, D, D, G]),
                                    k.unsqueeze(1).to_broadcast([P, D, D, G]), ALU.mult).then_inc(s_p1, 1)
                for t in range(TPB):
                    e.wait_ge(s_pr, TPB * b + t + 1)
                    v = qkv[:, t, 2 * DG:].rearrange("p (e g) -> p g e", g=G)
                    e.tensor_tensor(prod[:, t, :].rearrange("p (d g e) -> p d g e", d=D, g=G),
                                    sc[:, t].unsqueeze(2).to_broadcast([P, D, G, D]),
                                    v.unsqueeze(1).to_broadcast([P, D, G, D]), ALU.mult).then_inc(s_p2, 1)

        @block.tensor
        def _(e):
            e.wait_ge(s_cst, 3)
            e.wait_ge(s_wr, 2)
            e.wait_ge(s_w, 96)
            with e.Fori(0, B) as b:
                for t in range(TPB):
                    e.wait_ge(s_x[t], 16 * b + 16)
                    for c in range(C):
                        ins = e.transpose(tr[t][:, c, :], xt[:, t, c * P:(c + 1) * P], ident[:])
                    ins.then_inc(s_tr, 1)
                for t in range(TPB):
                    e.wait_ge(s_xT, TPB * b + t + 1)
                    for c in range(C):
                        e.matmul(pq[t][:, 0:3 * DG], xT[:, t, c, :], w[:, c, :], start=(c == 0), stop=False)
                    e.matmul(pq[t][:, 0:3 * DG], ones[:], bias[:], start=False, stop=True).then_inc(s_pq, 1)

        @block.scalar
        def _(e):
            e.preload_act_table_set("natural_log_exp_and_others")
            with e.Fori(0, B) as b:
                for t in range(TPB):
                    n = TPB * b + t + 1
                    e.wait_ge(s_tr, n)
                    e.activation(xT[:, t], tr[t][:], ACT.Copy).then_inc(s_xT, 1)
                for t in range(TPB):
                    n = TPB * b + t + 1
                    e.wait_ge(s_pq, n)
                    e.activation(qkv[:, t, :], pq[t][:, 0:3 * DG], ACT.Copy).then_inc(s_qkv, 1)
                for t in range(TPB):
                    n = TPB * b + t + 1
                    e.wait_ge(s_sh, n)
                    e.activation(sc[:, t], sc[:, t], ACT.Exp, scale=float(D) ** -0.5).then_inc(s_ex, 1)
                for t in range(TPB):
                    n = TPB * b + t + 1
                    e.wait_ge(s_va, n)
                    e.activation(rs[:, t, 1:2], rs[:, t, 0:1], ACT.Ln).then_inc(s_ln, 1)
                    e.wait_ge(s_ln, n)
                    e.activation(rs[:, t, 2:3], rs[:, t, 1:2], ACT.Exp, scale=-0.5).then_inc(s_y0, 1)

        @block.vector
        def _(e):
            e.wait_ge(s_w, 96)
            e.reduce_sum(w[:, :, 0:DG], w_raw[:].rearrange("p c (n r) -> p c n r", r=R), AX.X).then_inc(s_wr, 1)
            e.reduce_sum(bias[:, 0:DG], b_raw[:].rearrange("p (n r) -> p n r", r=R), AX.X).then_inc(s_wr, 1)
            with e.Fori(0, B) as b:
                def scores(t):
                    n = TPB * b + t + 1
                    e.wait_ge(s_p1, n)
                    e.reduce_sum(sc[:, t], prod[:, t, :].rearrange("p (d e g) -> p d e g", d=D, e=D), AX.X)\
                        .then_inc(s_sc, 1)
                    e.wait_ge(s_sc, n)
                    e.reduce_max(stat[:, t, 0, :], sc[:, t], AX.X).then_inc(s_mx, 1)
                    e.wait_ge(s_mx, n)
                    e.tensor_tensor(sc[:, t], sc[:, t], stat[:, t, 0, :].unsqueeze(2).to_broadcast([P, D, D]),
                                    ALU.subtract).then_inc(s_sh, 1)

                def normalise(t):
                    n = TPB * b + t + 1
                    e.wait_ge(s_ex, n)
                    e.reduce_sum(stat[:, t, 1, :], sc[:, t], AX.X).then_inc(s_su, 1)
                    e.wait_ge(s_su, n)
                    e.reciprocal(stat[:, t, 2, :], stat[:, t, 1, :]).then_inc(s_ri, 1)
                    e.wait_ge(s_ri, n)
                    e.tensor_tensor(sc[:, t], sc[:, t], stat[:, t, 2, :].unsqueeze(2).to_broadcast([P, D, D]),
                                    ALU.mult).then_inc(s_pr, 1)

                def residual(t):
                    n = TPB * b + t + 1
                    e.wait_ge(s_p2, n)
                    e.reduce_sum(o[:, t, :], prod[:, t, :].rearrange("p (n e) -> p n e", e=D), AX.X)\
                        .then_inc(s_o, 1)
                    e.wait_ge(s_o, n)
                    h = xt[:, t, :].rearrange("p (n r) -> p n r", r=R)
                    e.tensor_tensor(h, h, o[:, t, :].unsqueeze(2).to_broadcast([P, DG, R]), ALU.add)\
                        .then_inc(s_h, 1)
                    e.wait_ge(s_h, n)
                    e.bn_stats(bn[:, t, :], xt[:, t, :]).then_inc(s_bn, 1)
                    e.wait_ge(s_bn, 2 * n - 1)
                    e.sem_inc(s_go, 1)
                    e.bn_aggr(mv[:, t, :], bn[:, t, :]).then_inc(s_bn, 1)
                    e.wait_ge(s_bn, 2 * n)
                    e.tensor_scalar(rs[:, t, 0:1], mv[:, t, 1:2], 1e-5, None, ALU.add).then_inc(s_va, 1)

                def layernorm(t):
                    n = TPB * b + t + 1
                    e.wait_ge(s_y0, n)
                    newton_rsqrt(e, nc, rs[:, t, 0:1], rs[:, t, 2:3], rs[:, t, 3:4], rs[:, t, 4:5],
                                 (s_nw, 3 * n - 3)).then_inc(s_nw, 1)
                    e.wait_ge(s_nw, 3 * n)
                    e.tensor_scalar(xt[:, t, :], xt[:, t, :], mv[:, t, 0:1], rs[:, t, 4:5],
                                    ALU.subtract, ALU.mult).then_inc(s_x1, 1)

                for step in (scores, normalise, residual, layernorm):
                    for t in range(TPB):
                        step(t)


START, MID, TURN, LAST = "start", "mid", "turn", "last"


def cross_attention(nc, ctx_in, Wq, Wk, Wv, Wo, qw, kw, x1, y_out):
    B, L, E = ctx_in.shape
    S = x1.shape[1]
    HD = P
    KVH = Wk.shape[1] // HD
    GR = Wq.shape[1] // HD // KVH
    C = E // P
    TPB = S // P
    NK = L + S
    NJ = -(-NK // P)
    TAIL = NK - (NJ - 1) * P
    NKP = NJ * P
    NQ = GR * TPB
    CH = [(c * 512, min(512, NK - c * 512)) for c in range(-(-NK // 512))]
    CH = [(o, n + n % 2) for o, n in CH]
    SETS = [list(range(4 * s, min(4 * s + 4, NJ))) for s in range(-(-NJ // 4))]
    assert TPB == 2 and GR == 4 and C == 4 and len(CH) == 4 and len(SETS) == 4 and NQ == 8
    SPLIT = 1024
    H1 = 8
    EPS = 1e-6

    X_IN_STEP = {i: [n for n in range(NJ) if n * (NQ - 1) // NJ + 1 == i] for i in range(1, NQ)}

    def ring_order(kind):
        order = []
        if kind == START:
            order += [("X", n) for n in range(NJ)]
        else:
            for i in range(1, NQ):
                order += [("T", i - 1, s) for s in range(4)]
                if kind == TURN:
                    order += [("X", n) for n in X_IN_STEP[i]]
            order += [("T", NQ - 1, s) for s in range(4)]
        if kind == LAST:
            return order + [("O", 0), ("O", 1)]
        order += [("KT", 0), ("KT", 1), ("Q", 0), ("Q", 1), ("QT", 0), ("QT", 1), ("KT", 2)]
        if kind != START:
            order += [("O", 0)]
        order += [("KT", 3)]
        if kind != START:
            order += [("O", 1)]
        return order

    RING = {k: ring_order(k) for k in (START, MID, TURN, LAST)}
    HI = {k: [x for x in v if x[0] in ("X", "T", "KT", "QT")] for k, v in RING.items()}
    assert len(RING[MID]) % 3 == 0 and len(RING[TURN]) % 3 == 0

    class Unit:

        def __init__(self, kind, b, h):
            self.kind, self.b, self.h = kind, b, h
            self.u = -1 if kind == START else b * KVH + h

            def before(table):
                if kind == START:
                    return 0
                per_batch = (KVH - 1) * len(table[MID]) + len(table[TURN])
                return len(table[START]) + b * per_batch + h * len(table[MID])
            self.ring0, self.hi0 = before(RING), before(HI)

        def ring(self, *label):
            return self.ring0 + RING[self.kind].index(label) + 1

        def hi(self, *label):
            return self.hi0 + HI[self.kind].index(label) + 1

        def bank(self, *label):
            first = 0 if self.kind == START else len(RING[START])
            return (first + RING[self.kind].index(label)) % 3

        def has_next(self):
            return self.kind != LAST

    def units(e, body):
        body(Unit(START, 0, 0))
        with e.Fori(0, B - 1) as b:
            with e.Fori(0, KVH - 1) as h:
                body(Unit(MID, b, h))
            body(Unit(TURN, b, KVH - 1))
        with e.Fori(0, KVH - 1) as h:
            body(Unit(MID, B - 1, h))
        body(Unit(LAST, B - 1, KVH - 1))

    with ExitStack() as ctx:
        def sb(name, shape, dt=F32):
            return ctx.enter_context(nc.sbuf_tensor(name, shape, dt))

        def sem(name):
            return ctx.enter_context(nc.semaphore(name))

        def pair(name, shape):
            return sb(name + "_hi", shape, F32R), sb(name + "_lo", shape, F32R)

        kvT_hi, kvT_lo = pair("kvT", [P, C, NKP])
        KT_hi, KT_lo = pair("KT", [P, NKP])
        V_hi, V_lo = pair("V", [P, NJ, HD])
        PT_hi, PT_lo = pair("PT", [P, NJ, TPB * P])
        QT_hi, QT_lo = pair("QT", [P, GR, TPB * P])
        OT_hi, OT_lo = pair("OT", [P, GR, TPB * P])
        Wkv_hi, Wkv_lo = pair("Wkv", [P, C, 2 * HD])
        Wq_hi, Wq_lo = pair("Wq", [P, C, GR * HD])
        Wo_hi, Wo_lo = pair("Wo", [P, GR, E])
        stage = sb("w_stage", [P, 1024])
        prob = sb("prob", [P, 2, NKP])
        nat = sb("nat", [P, 2, 4, HD])
        y = sb("y", [P, TPB, E])
        ident = sb("ident", [P, P])
        one = sb("one", [P, 1])
        qkw = sb("qkw", [P, 3])
        pm = sb("pm", [P, 2, 3])
        nm = sb("nm", [P, 2])
        rsum = sb("rsum", [P, 2, 2])
        rinv = sb("rinv", [P, 2, 2])
        nrm = sb("nrm", [P, 6, 4])

        S_ps = ctx.enter_context(nc.psum_tensor("S_ps", [P, 4 * 512], F32))
        ring_ps = [ctx.enter_context(nc.psum_tensor(f"ring{i}", [P, 512], F32)) for i in range(3)]
        OT_ps = ctx.enter_context(nc.psum_tensor("OT_ps", [P, 512], F32))
        KV_ps = S_ps[:].rearrange("p (a n) -> p a n", n=2 * HD)

        s_id = sem("identity")
        s_pad = sem("pads_zeroed")
        s_qkw = sem("norm_weights_loaded")
        s_w = sem("norm_weight_ready")
        s_wd = sem("weights_loaded")
        s_ws = sem("weights_split")
        s_xd = [sem(f"key_rows_loaded{i}") for i in range(2)]
        s_yd = sem("y_moved")
        s_full = sem("ring_full")
        s_free = sem("ring_free")
        s_hi = sem("ring_hi_copied")
        s_sc = sem("scores_full")
        s_max = sem("chunk_max")
        s_nm = sem("negated_max")
        s_exp = sem("exponentials")
        s_rs = sem("row_sum")
        s_ri = sem("row_reciprocal")
        s_pn = sem("left_probabilities_normed")
        s_pa = sem("right_probabilities_normed")
        s_of = sem("OT_full")
        s_oh = sem("OT_hi_copied")
        s_ol = sem("OT_lo_copied")
        s_kv = sem("KV_full")
        s_sq = sem("squares")
        s_ss = sem("sum_of_squares")
        s_ms = sem("mean_square")
        s_ln = sem("log_mean_square")
        s_y0 = sem("rsqrt_estimate")
        s_nw = sem("newton_steps")
        s_nat = sem("rows_normed")
        s_vh = sem("V_hi_copied")
        s_vl = sem("V_lo_copied")

        block = ctx.enter_context(nc.Block())

        def target(label, bank):
            ps = ring_ps[bank][:]
            if label[0] == "T":
                _, i, s = label
                n, q = len(SETS[s]), (i % TPB) * P
                return (ps[:, 0:n * P].rearrange("p (j q) -> p j q", q=P),
                        PT_hi[:, 4 * s:4 * s + n, q:q + P], PT_lo[:, 4 * s:4 * s + n, q:q + P])
            if label[0] == "KT":
                n = len(SETS[label[1]]) * P
                at = label[1] * 512
                return ps[:, 0:n], KT_hi[:, at:at + n], KT_lo[:, at:at + n]
            if label[0] == "QT":
                q = label[1] * P
                return (ps.rearrange("p (h q) -> p h q", q=P), QT_hi[:, :, q:q + P], QT_lo[:, :, q:q + P])
            n = label[1]
            rows = P if n < NJ - 1 else TAIL
            return (ps.rearrange("p (c k) -> p c k", k=P)[:, :, 0:rows],
                    kvT_hi[:, :, n * P:n * P + rows], kvT_lo[:, :, n * P:n * P + rows])

        JOBS = [("KV", 0), ("KV", 1), ("Q", 0), ("Q", 1), ("KV", 2), ("KV", 3)]
        OUT = {("KV", g): ("KT", g) for g in range(4)} | {("Q", t): ("QT", t) for t in range(TPB)}

        def job_no(U, job):
            return 6 * (U.u + 1) + JOBS.index(job) + 1

        def job_source(U, job):
            if job[0] == "Q":
                return ring_ps[U.bank(*job)][:].rearrange("p (h d) -> p h d", d=HD)
            g = job[1]
            a = 4 * (g % 2)
            return KV_ps[:, a:a + len(SETS[g]), 0:HD]

        def v_source(g):
            a = 4 * (g % 2)
            return KV_ps[:, a:a + len(SETS[g]), HD:2 * HD]

        def weights_split(U, n):
            return 2 * n if U.kind == START else 2 * (3 + 5 * U.u + n)

        @block.sync
        def _(e):
            e.dma_start(qkw[:, 0:1], qw.rearrange("(p o) -> p o", o=1)).then_inc(s_qkw, 16)
            e.dma_start(qkw[:, 1:2], kw.rearrange("(p o) -> p o", o=1)).then_inc(s_qkw, 16)
            e.dma_start(y[:], x1[0].rearrange("(t p) e -> p t e", p=P)).then_inc(s_yd, 16)
            wk = Wk.rearrange("(c p) n -> p c n", p=P)
            wv = Wv.rearrange("(c p) n -> p c n", p=P)
            wq = Wq.rearrange("(c p) n -> p c n", p=P)
            wo = Wo.rearrange("(g p) n -> p g n", p=P)

            def body(U):
                job = 0

                def free(n):
                    if not (U.kind == START and n == 0):
                        e.wait_ge(s_ws, weights_split(U, n))
                if U.has_next():
                    h = 0 if U.kind in (START, TURN) else U.h + 1
                    st = stage[:].rearrange("p (c n) -> p c n", c=C)
                    free(0)
                    e.dma_start(st[:, :, 0:HD], wk[:, :, bass.ts(h, HD)]).then_inc(s_wd, 16)
                    e.dma_start(st[:, :, HD:2 * HD], wv[:, :, bass.ts(h, HD)]).then_inc(s_wd, 16)
                    for a in range(2):
                        free(1 + a)
                        e.dma_start(stage[:].rearrange("p (c n) -> p c n", c=2),
                                    wq[:, 2 * a:2 * a + 2, bass.ts(h, GR * HD)]).then_inc(s_wd, 16)
                    job = 3
                if U.kind != START:
                    for a in range(2):
                        free(job + a)
                        e.dma_start(stage[:].rearrange("p (c n) -> p c n", c=2),
                                    wo[:, bass.ds(U.h * GR + 2 * a, 2), :]).then_inc(s_wd, 16)
                if U.kind in (TURN, LAST):
                    e.wait_ge(s_free, U.ring("O", 1))
                    e.dma_start(y_out[bass.ds(U.b, 1)].rearrange("o (t p) e -> p (o t) e", p=P), y[:])\
                        .then_inc(s_yd, 16)
                    e.wait_ge(s_yd, 32 * U.b + 32)
                if U.kind == TURN:
                    e.dma_start(y[:], x1[bass.ds(U.b + 1, 1)].rearrange("o (t p) e -> p (o t) e", p=P))\
                        .then_inc(s_yd, 16)
            units(e, body)

        @block.gpsimd
        def _(e):
            e.sem_inc(s_ol, 1)
            e.memset(ident[:], 0.0).then_inc(s_id, 1)
            e.wait_ge(s_id, 1)
            e.affine_select(out=ident[:], in_=ident[:], compare_op=ALU.not_equal, fill=1.0, base=0,
                            pattern=[[-1, P]], channel_multiplier=1).then_inc(s_id, 1)
            e.memset(one[:], 1.0).then_inc(s_id, 1)
            e.memset(f(kvT_hi[:, :, NK:NKP]), 0.0).then_inc(s_pad, 1)
            e.memset(f(kvT_lo[:, :, NK:NKP]), 0.0).then_inc(s_pad, 1)
            e.memset(prob[:, :, NK:NKP], 0.0).then_inc(s_pad, 1)

            def body(U):
                dmas = 0 if U.kind == START else 16 * (4 + 6 * U.u)
                n = 0
                if U.kind == START:
                    e.wait_ge(s_id, 3)
                else:
                    e.wait_ge(s_full, U.ring0)

                def split(src, hi, lo, loads):
                    nonlocal dmas, n
                    dmas = dmas + 16 * loads
                    e.wait_ge(s_wd, dmas)
                    e.tensor_tensor(hi, src, one[:].unsqueeze(2).to_broadcast(list(src.shape)), ALU.mult).then_inc(s_ws, 1)
                    e.wait_ge(s_ws, weights_split(U, n) + 1)
                    e.tensor_tensor(lo, src, f(hi), ALU.subtract).then_inc(s_ws, 1)
                    n += 1
                if U.has_next():
                    split(stage[:].rearrange("p (c n) -> p c n", c=C), Wkv_hi[:], Wkv_lo[:], 2)
                    for a in range(2):
                        split(stage[:].rearrange("p (c n) -> p c n", c=2),
                              Wq_hi[:, 2 * a:2 * a + 2, :], Wq_lo[:, 2 * a:2 * a + 2, :], 1)
                if U.kind != START:
                    for a in range(2):
                        split(stage[:].rearrange("p (c n) -> p c n", c=2),
                              Wo_hi[:, 2 * a:2 * a + 2, :], Wo_lo[:, 2 * a:2 * a + 2, :], 1)
            units(e, body)

        @block.tensor
        def _(e):
            e.wait_ge(s_id, 2)
            e.wait_ge(s_pad, 3)

            def three(out, l_hi, l_lo, r_hi, r_lo, first, last):
                e.matmul(out, l_hi, r_hi, start=first, stop=False)
                e.matmul(out, l_hi, r_lo, start=False, stop=False)
                return e.matmul(out, l_lo, r_hi, start=False, stop=last)

            def body(U):
                u = U.u

                def take(*label):
                    if not (U.kind == START and RING[START].index(label) < 3):
                        e.wait_ge(s_free, U.ring(*label) - 3)
                    return ring_ps[U.bank(*label)][:]

                def rows_in(n):
                    before = 0 if U.kind == START else (U.b + 1) * len(range(n % 2, NJ, 2))
                    e.wait_ge(s_xd[n % 2], 16 * (before + n // 2 + 1))
                    ps = take("X", n)
                    rows = P if n < NJ - 1 else TAIL
                    for c in range(C):
                        ins = e.transpose(ps[:, c * P:c * P + rows], nat[0:rows, n % 2, c, :],
                                          ident[0:rows, 0:rows])
                    ins.then_inc(s_full, 1)

                def scores(i, c):
                    at, n = CH[c]
                    g, q = i % NQ // TPB, (i % TPB) * P
                    if i == NQ:
                        if c == 0:
                            e.wait_ge(s_free, U.ring("KT", 1))
                            e.wait_ge(s_free, U.ring("QT", 1))
                            e.wait_ge(s_nat, job_no(U, ("KV", 2)))
                            e.wait_ge(s_vl, 4 * (u + 1) + 3)
                        elif c == 2:
                            e.wait_ge(s_free, U.ring("KT", 2))
                            e.wait_ge(s_nat, job_no(U, ("KV", 3)))
                            e.wait_ge(s_vl, 4 * (u + 1) + 4)
                        elif c == 3:
                            e.wait_ge(s_free, U.ring("KT", 3))
                    elif c <= 1:
                        e.wait_ge(s_exp, 2 * (NQ * u + i - 1) + 1 + c)
                    three(S_ps[:, c * 512:c * 512 + n], QT_hi[:, g, q:q + P], QT_lo[:, g, q:q + P],
                          KT_hi[:, at:at + n], KT_lo[:, at:at + n], True, True).then_inc(s_sc, 1)

                def turn(i, s):
                    if s == 0:
                        e.wait_ge(s_pn, NQ * u + i + 1)
                        e.wait_ge(s_pa, NQ * u + i + 1)
                    ps = take("T", i, s)
                    for k, j in enumerate(SETS[s]):
                        ins = e.transpose(ps[:, k * P:(k + 1) * P], prob[:, i % 2, j * P:(j + 1) * P], ident[:])
                    ins.then_inc(s_full, 1)

                def pv(g, js):
                    for j in js:
                        if j == 0:
                            e.wait_ge(s_ol, GR * u + g + 1)
                        if j % 4 == 0:
                            e.wait_ge(s_free, U.ring("T", TPB * g + 1, j // 4))
                        ins = three(OT_ps[:, 0:TPB * P], V_hi[:, j, :], V_lo[:, j, :],
                                    PT_hi[:, j, :], PT_lo[:, j, :], j == 0, j == NJ - 1)
                    if js[-1] == NJ - 1:
                        ins.then_inc(s_of, 1)

                def kv(g, ks):
                    if ks[0] == SETS[g][0]:
                        if g == 0:
                            e.wait_ge(s_ws, weights_split(U, 1))
                        if g < 2:
                            if U.kind == START:
                                e.wait_ge(s_free, NJ)
                            else:
                                e.wait_ge(s_exp, 2 * NQ * (u + 1))
                                if U.kind == TURN:
                                    e.wait_ge(s_free, U.ring("X", NJ - 1))
                        else:
                            e.wait_ge(s_nat, job_no(U, ("KV", g - 2)))
                            e.wait_ge(s_vl, 4 * (u + 1) + g - 1)
                    for j in ks:
                        out = KV_ps[:, 4 * (g % 2) + j % 4, :]
                        for c in range(C):
                            ins = three(out, kvT_hi[:, c, j * P:(j + 1) * P], kvT_lo[:, c, j * P:(j + 1) * P],
                                        Wkv_hi[:, c, :], Wkv_lo[:, c, :], c == 0, c == C - 1)
                    if ks[-1] == SETS[g][-1]:
                        ins.then_inc(s_kv, 1)

                def queries(t):
                    if t == 0:
                        e.wait_ge(s_ws, weights_split(U, 3))
                    ps = take("Q", t)
                    for c in range(C):
                        ins = three(ps, kvT_hi[:, c, t * P:(t + 1) * P], kvT_lo[:, c, t * P:(t + 1) * P],
                                    Wq_hi[:, c, :], Wq_lo[:, c, :], c == 0, c == C - 1)
                    ins.then_inc(s_full, 1)

                def rows_out(job):
                    e.wait_ge(s_nat, job_no(U, job))
                    ps = take(*OUT[job])
                    n = GR if job[0] == "Q" else len(SETS[job[1]])
                    for k in range(n):
                        ins = e.transpose(ps[:, k * P:(k + 1) * P], nat[:, JOBS.index(job) % 2, k, :], ident[:])
                    ins.then_inc(s_full, 1)

                def output(t):
                    if t == 0:
                        e.wait_ge(s_ws, weights_split(U, 5 if U.has_next() else 2))
                        e.wait_ge(s_ol, GR * (u + 1) + 1)
                    ps = take("O", t)
                    for g in range(GR):
                        ins = three(ps, OT_hi[:, g, t * P:(t + 1) * P], OT_lo[:, g, t * P:(t + 1) * P],
                                    Wo_hi[:, g, :], Wo_lo[:, g, :], g == 0, g == GR - 1)
                    ins.then_inc(s_full, 1)

                first_half, rest = list(range(H1)), list(range(H1, NJ))
                if U.kind == START:
                    for n in range(NJ):
                        rows_in(n)
                    for g in range(2):
                        kv(g, SETS[g])
                        rows_out(("KV", g))
                else:
                    for i in range(1, NQ):
                        g = i // TPB - 1
                        scores(i, 0)
                        scores(i, 1)
                        turn(i - 1, 0)
                        scores(i, 2)
                        turn(i - 1, 1)
                        scores(i, 3)
                        if i % 2 == 0:
                            turn(i - 1, 2)
                            turn(i - 1, 3)
                            pv(g, first_half)
                        else:
                            if g >= 0:
                                pv(g, rest[:4])
                            turn(i - 1, 2)
                            if g >= 0:
                                pv(g, rest[4:])
                            turn(i - 1, 3)
                        if U.kind == TURN:
                            for n in X_IN_STEP[i]:
                                rows_in(n)
                    i = NQ - 1
                    if U.has_next():
                        kv(0, SETS[0][0:2])
                    turn(i, 0)
                    turn(i, 1)
                    if U.has_next():
                        kv(0, SETS[0][2:4])
                    turn(i, 2)
                    turn(i, 3)
                    if U.has_next():
                        kv(1, SETS[1])
                        rows_out(("KV", 0))
                    pv(GR - 1, first_half + rest)
                    if U.has_next():
                        rows_out(("KV", 1))
                if U.has_next():
                    queries(0)
                    queries(1)
                    kv(2, SETS[2])
                    rows_out(("Q", 0))
                    rows_out(("Q", 1))
                    kv(3, SETS[3])
                    rows_out(("KV", 2))
                    scores(NQ, 0)
                    scores(NQ, 1)
                if U.kind != START:
                    output(0)
                if U.has_next():
                    rows_out(("KV", 3))
                    scores(NQ, 2)
                    scores(NQ, 3)
                if U.kind != START:
                    output(1)
            units(e, body)

        @block.scalar
        def _(e):
            e.preload_act_table_set("natural_log_exp_and_others")
            e.wait_ge(s_pad, 3)

            def body(U):
                u = U.u

                def load_rows(n):
                    rows = P if n < NJ - 1 else TAIL
                    b = 0 if U.kind == START else U.b + 1
                    if n < TPB:
                        src = x1[bass.ds(b, 1), n * P:n * P + rows, :]
                    else:
                        src = ctx_in[bass.ds(b, 1), (n - TPB) * P:(n - TPB) * P + rows, :]
                    if n >= 2:
                        e.wait_ge(s_full, U.ring("X", n - 2))
                    elif U.kind != START:
                        e.wait_ge(s_full, U.ring0)
                    e.dma_start(nat[0:rows, n % 2].rearrange("p c d -> p (c d)"),
                                src.rearrange("o p e -> (o p) e")).then_inc(s_xd[n % 2], 16)

                def hi(*label):
                    ps, dst, _ = target(label, U.bank(*label))
                    e.wait_ge(s_full, U.ring(*label))
                    if label[0] == "QT":
                        e.activation(dst, ps, ACT.Copy, scale=qkw[:, 2:3]).then_inc(s_hi, 1)
                    else:
                        e.activation(dst, ps, ACT.Copy).then_inc(s_hi, 1)
                    if label[0] == "X" and label[1] + 2 < NJ:
                        load_rows(label[1] + 2)

                def norm(i):
                    e.wait_ge(s_ri, NQ * u + i + 1)
                    p = prob[:, i % 2, SPLIT:NK]
                    e.activation(p, p, ACT.Copy, scale=rinv[:, i % 2, 1:2]).then_inc(s_pa, 1)

                def exps(i, half):
                    at, to = ((0, 512), (512, NK))[half]
                    if half == 0:
                        e.wait_ge(s_nm, NQ * u + i + 1)
                    if half == 0 and i != 1 and U.kind != START:
                        e.wait_ge(s_full, U.ring("T", i - 2, 3))
                    e.activation(prob[:, i % 2, at:to], S_ps[:, at:to], ACT.Exp, bias=nm[:, i % 2:i % 2 + 1],
                                 accum_out=rsum[:, i % 2, half:half + 1]).then_inc(s_exp, 1)

                def out_hi(g):
                    e.wait_ge(s_of, GR * u + g + 1)
                    e.activation(OT_hi[:, g, :], OT_ps[:, 0:TPB * P], ACT.Copy).then_inc(s_oh, 1)

                def squares(job):
                    no = JOBS.index(job)
                    n = job_no(U, job)
                    if job[0] == "Q":
                        e.wait_ge(s_full, U.ring(*job))
                    else:
                        e.wait_ge(s_kv, 4 * (u + 1) + job[1] + 1)
                    if no >= 2:
                        e.wait_ge(s_full, U.ring(*OUT[JOBS[no - 2]]))
                    src = job_source(U, job)
                    k = src.shape[1]
                    e.activation(nat[:, no % 2, 0:k, :], src, ACT.Square).then_inc(s_sq, 1)
                    e.wait_ge(s_ms, n)
                    e.activation(nrm[:, 2, 0:k], nrm[:, 1, 0:k], ACT.Ln).then_inc(s_ln, 1)
                    e.wait_ge(s_ln, n)
                    e.activation(nrm[:, 3, 0:k], nrm[:, 2, 0:k], ACT.Exp, scale=-0.5).then_inc(s_y0, 1)

                def v_hi(g):
                    e.wait_ge(s_nat, job_no(U, ("KV", g)))
                    if g < 2 and U.kind != START:
                        e.wait_ge(s_of, GR * (u + 1))
                    e.activation(V_hi[:, 4 * g:4 * g + len(SETS[g]), :], v_source(g), ACT.Copy).then_inc(s_vh, 1)

                if U.kind == START:
                    load_rows(0)
                    load_rows(1)
                    for n in range(NJ):
                        hi("X", n)
                    e.wait_ge(s_w, 1)
                    for g in range(2):
                        squares(("KV", g))
                        hi("KT", g)
                    v_hi(0)
                    v_hi(1)
                else:
                    if U.kind == TURN:
                        load_rows(0)
                        load_rows(1)
                    norm(0)
                    for i in range(1, NQ):
                        hi("T", i - 1, 0)
                        hi("T", i - 1, 1)
                        if i % 2 == 0:
                            hi("T", i - 1, 2)
                            exps(i, 0)
                            exps(i, 1)
                            hi("T", i - 1, 3)
                            norm(i)
                        else:
                            exps(i, 0)
                            exps(i, 1)
                            hi("T", i - 1, 2)
                            norm(i)
                            hi("T", i - 1, 3)
                        if i % 2 and i >= 3:
                            out_hi((i - 3) // 2)
                        if U.kind == TURN:
                            for n in X_IN_STEP[i]:
                                hi("X", n)
                    i = NQ - 1
                    hi("T", i, 0)
                    hi("T", i, 1)
                    if U.has_next():
                        squares(("KV", 0))
                    hi("T", i, 2)
                    hi("T", i, 3)
                    if U.has_next():
                        squares(("KV", 1))
                        hi("KT", 0)
                    out_hi(GR - 1)
                    if U.has_next():
                        v_hi(0)
                        v_hi(1)
                        hi("KT", 1)
                if U.has_next():
                    squares(("Q", 0))
                    squares(("Q", 1))
                    hi("QT", 0)
                    hi("QT", 1)
                    squares(("KV", 2))
                    v_hi(2)
                    hi("KT", 2)
                    squares(("KV", 3))
                    v_hi(3)
                    hi("KT", 3)
                    exps(NQ, 0)
                    exps(NQ, 1)
            units(e, body)

        @block.vector
        def _(e):
            e.wait_ge(s_qkw, 32)
            e.scalar_tensor_tensor(qkw[:, 2:3], qkw[:, 0:1], float(HD) ** -0.5, qkw[:, 1:2],
                                   ALU.mult, ALU.mult).then_inc(s_w, 1)
            e.wait_ge(s_w, 1)
            e.wait_ge(s_pad, 3)

            def body(U):
                u = U.u

                def lo(*label):
                    ps, hi, dst = target(label, U.bank(*label))
                    e.wait_ge(s_hi, U.hi(*label))
                    if label[0] == "QT":
                        e.scalar_tensor_tensor(dst, ps, qkw[:, 2:3], f(hi), ALU.mult, ALU.subtract)\
                            .then_inc(s_free, 1)
                    else:
                        e.tensor_tensor(dst, ps, f(hi), ALU.subtract).then_inc(s_free, 1)

                def chunk_max(i, k):
                    at, to, c = ((0, 1024, 1), (1024, 1536, 2), (1536, NK, 3))[k]
                    e.wait_ge(s_sc, 4 * (NQ * u + i) + c + 1)
                    e.reduce_max(pm[:, i % 2, k:k + 1], S_ps[:, at:to], AX.X).then_inc(s_max, 1)

                def negate(i):
                    e.wait_ge(s_max, 3 * (NQ * u + i + 1))
                    e.tensor_reduce(nm[:, i % 2:i % 2 + 1], pm[:, i % 2, :], AX.X, ALU.max, negate=True)\
                        .then_inc(s_nm, 1)

                def norm_rows(i):
                    e.wait_ge(s_ri, NQ * u + i + 1)
                    p = prob[:, i % 2, 0:SPLIT]
                    e.tensor_scalar(p, p, rinv[:, i % 2, 1:2], None, ALU.mult).then_inc(s_pn, 1)

                def reciprocal(i):
                    e.wait_ge(s_exp, 2 * (NQ * u + i + 1))
                    e.tensor_tensor(rinv[:, i % 2, 0:1], rsum[:, i % 2, 0:1], rsum[:, i % 2, 1:2], ALU.add)\
                        .then_inc(s_rs, 1)
                    e.wait_ge(s_rs, NQ * u + i + 1)
                    e.reciprocal(rinv[:, i % 2, 1:2], rinv[:, i % 2, 0:1]).then_inc(s_ri, 1)

                def out_lo(g):
                    e.wait_ge(s_oh, GR * u + g + 1)
                    e.tensor_tensor(OT_lo[:, g, :], OT_ps[:, 0:TPB * P], f(OT_hi[:, g, :]), ALU.subtract)\
                        .then_inc(s_ol, 1)

                def norm(job):
                    no = JOBS.index(job)
                    n = job_no(U, job)
                    src = job_source(U, job)
                    k = src.shape[1]
                    rows = nat[:, no % 2, 0:k, :]
                    e.wait_ge(s_sq, n)
                    e.reduce_sum(nrm[:, 0, 0:k], rows, AX.X).then_inc(s_ss, 1)
                    e.wait_ge(s_ss, n)
                    e.tensor_scalar(nrm[:, 1, 0:k], nrm[:, 0, 0:k], 1.0 / HD, EPS, ALU.mult, ALU.add)\
                        .then_inc(s_ms, 1)
                    e.wait_ge(s_y0, n)
                    newton_rsqrt(e, nc, nrm[:, 1, 0:k], nrm[:, 3, 0:k], nrm[:, 4, 0:k], nrm[:, 5, 0:k],
                                 (s_nw, 3 * n - 3)).then_inc(s_nw, 1)
                    e.wait_ge(s_nw, 3 * n)
                    e.tensor_tensor(rows, src, nrm[:, 5, 0:k].unsqueeze(2).to_broadcast([P, k, HD]),
                                    ALU.mult).then_inc(s_nat, 1)
                    if job[0] == "Q":
                        e.wait_ge(s_nat, n)
                        e.sem_inc(s_free, 1)

                def v_lo(g):
                    e.wait_ge(s_vh, 4 * (u + 1) + g + 1)
                    at = slice(4 * g, 4 * g + len(SETS[g]))
                    e.tensor_tensor(V_lo[:, at, :], v_source(g), f(V_hi[:, at, :]), ALU.subtract)\
                        .then_inc(s_vl, 1)

                def add_output(t):
                    e.wait_ge(s_full, U.ring("O", t))
                    if t == 0:
                        e.wait_ge(s_yd, 32 * U.b + 16)
                    e.tensor_tensor(y[:, t, :], y[:, t, :], ring_ps[U.bank("O", t)][:], ALU.add)\
                        .then_inc(s_free, 1)

                if U.kind == START:
                    for n in range(NJ):
                        lo("X", n)
                    for g in range(2):
                        norm(("KV", g))
                        lo("KT", g)
                    v_lo(0)
                    v_lo(1)
                else:
                    norm_rows(0)
                    for i in range(1, NQ):
                        chunk_max(i, 0)
                        if i % 2 == 0:
                            lo("T", i - 1, 0)
                        chunk_max(i, 1)
                        chunk_max(i, 2)
                        negate(i)
                        if i % 2:
                            lo("T", i - 1, 0)
                        lo("T", i - 1, 1)
                        if i % 2 == 0:
                            lo("T", i - 1, 2)
                        reciprocal(i)
                        norm_rows(i)
                        if i % 2:
                            lo("T", i - 1, 2)
                        lo("T", i - 1, 3)
                        if i % 2 and i >= 3:
                            out_lo((i - 3) // 2)
                        if U.kind == TURN:
                            for n in X_IN_STEP[i]:
                                lo("X", n)
                    i = NQ - 1
                    lo("T", i, 0)
                    lo("T", i, 1)
                    if U.has_next():
                        norm(("KV", 0))
                    lo("T", i, 2)
                    lo("T", i, 3)
                    if U.has_next():
                        norm(("KV", 1))
                        lo("KT", 0)
                    out_lo(GR - 1)
                    if U.has_next():
                        v_lo(0)
                        v_lo(1)
                        lo("KT", 1)
                if U.has_next():
                    norm(("Q", 0))
                    norm(("Q", 1))
                    lo("QT", 0)
                    lo("QT", 1)
                    norm(("KV", 2))
                    v_lo(2)
                    lo("KT", 2)
                    norm(("KV", 3))
                    v_lo(3)
                    if U.kind != START:
                        add_output(0)
                    chunk_max(NQ, 0)
                    lo("KT", 3)
                    chunk_max(NQ, 1)
                    chunk_max(NQ, 2)
                    negate(NQ)
                    if U.kind != START:
                        add_output(1)
                    reciprocal(NQ)
                else:
                    add_output(0)
                    add_output(1)
            units(e, body)


def feed_forward(nc, y_in, Wr, rb, eb, out):
    B, S, E = y_in.shape
    NE = Wr.shape[0]
    C = E // P
    TPB = S // P
    TOP = 8

    with ExitStack() as ctx:
        def sb(name, shape, dt=F32):
            return ctx.enter_context(nc.sbuf_tensor(name, shape, dt))

        def sem(name):
            return ctx.enter_context(nc.semaphore(name))

        N = B * TPB

        def first_norm(n):
            return max(2 * n - 1, 0)

        def last_norm(n):
            return min(2 * n + 2, 2 * N - 1)

        y = sb("f_y", [P, N, E])
        z = sb("f_z", [P, N, E])
        xT = sb("f_xT", [P, 2, C, P])
        wr = sb("f_wr", [NE, E])
        wrT = sb("f_wrT", [P, C, NE])
        ebs = sb("f_eb", [NE, E])
        rbs = sb("f_rb", [1, NE])
        ones = sb("f_ones", [1, P])
        ident = sb("f_ident", [P, P])
        bn = sb("f_bn", [P, N, 6])
        mv = sb("f_mv", [P, N, 2])
        rs = sb("f_rs", [P, N, 5])
        soft = sb("f_soft", [P, N, 4])
        ex = sb("f_exp", [P, N, NE])
        rest = sb("f_rest", [P, N, NE])
        top = sb("f_top", [P, N, TOP])
        wT = sb("f_wT", [NE, 2, P])
        tr = [ctx.enter_context(nc.psum_tensor(f"f_tr{i}", [P, 512], F32)) for i in range(2)]
        lg = [ctx.enter_context(nc.psum_tensor(f"f_lg{i}", [P, 512], F32)) for i in range(2)]
        tw = [ctx.enter_context(nc.psum_tensor(f"f_tw{i}", [P, 512], F32)) for i in range(2)]
        mx = [ctx.enter_context(nc.psum_tensor(f"f_mx{i}", [P, 512], F32)) for i in range(2)]

        s_w = sem("f_weights_loaded")
        s_c = sem("f_constants")
        s_y = [sem(f"f_y_loaded{n}") for n in range(N)]
        s_wt = sem("f_router_transposed")
        s_wc = sem("f_router_copied")
        s_bn = sem("f_bn_steps")
        s_va = sem("f_variance")
        s_ln = sem("f_log_variance")
        s_y0 = sem("f_rsqrt_estimate")
        s_nw = sem("f_newton_steps")
        s_x2 = sem("f_x2")
        s_tr = sem("f_x2_transposed")
        s_xT = sem("f_x2T_copied")
        s_lg = sem("f_logits")
        s_nm = sem("f_negated_max")
        s_ex = sem("f_exponentials")
        s_sm = sem("f_softmax_steps")
        s_tk = sem("f_top_weights")
        s_tw = sem("f_weights_transposed")
        s_tc = sem("f_weights_copied")
        s_mx = sem("f_mixed")
        s_z = sem("f_z")
        s_ou = sem("f_normed")
        s_st = sem("f_stored")

        block = ctx.enter_context(nc.Block())
        yv = y_in.rearrange("b (t p) e -> p (b t) e", p=P)
        ov = out.rearrange("b (t p) e -> p (b t) e", p=P)

        @block.sync
        def _(e):
            e.dma_start(y[:, 0, :], yv[:, 0, :]).then_inc(s_y[0], 16)
            e.dma_start(wr[:], Wr).then_inc(s_w, 16)
            e.dma_start(ebs[:], eb).then_inc(s_w, 16)
            e.dma_start(rbs[:], rb.rearrange("(o n) -> o n", o=1)).then_inc(s_w, 16)
            for n in range(1, N):
                e.dma_start(y[:, n, :], yv[:, n, :]).then_inc(s_y[n], 16)
            for n in range(N):
                e.wait_ge(s_ou, n + 1)
                e.dma_start(ov[:, n, :], z[:, n, :]).then_inc(s_st, 16)
            e.wait_ge(s_st, 16 * N)

        @block.gpsimd
        def _(e):
            e.memset(ones[:], 1.0).then_inc(s_c, 1)
            e.memset(ident[:], 0.0).then_inc(s_c, 1)
            e.wait_ge(s_c, 2)
            e.affine_select(out=ident[:], in_=ident[:], compare_op=ALU.not_equal, fill=1.0, base=0,
                            pattern=[[-1, P]], channel_multiplier=1).then_inc(s_c, 1)

        @block.tensor
        def _(e):
            e.wait_ge(s_c, 3)
            e.wait_ge(s_w, 48)
            for c in range(C):
                ins = e.transpose(tw[0][:, c * NE:(c + 1) * NE], wr[:, c * P:(c + 1) * P], ident[0:NE, 0:NE])
            ins.then_inc(s_wt, 1)
            e.wait_ge(s_wc, 1)

            def logits(n):
                e.wait_ge(s_x2, n + 1)
                for c in range(C):
                    ins = e.transpose(tr[n % 2][:, c * P:(c + 1) * P], y[:, n, c * P:(c + 1) * P], ident[:])
                ins.then_inc(s_tr, 1)
                e.wait_ge(s_xT, n + 1)
                for c in range(C):
                    e.matmul(lg[n % 2][:, 0:NE], xT[:, n % 2, c, :], wrT[:, c, :], start=(c == 0), stop=False)
                e.matmul(lg[n % 2][:, 0:NE], ones[:], rbs[:], start=False, stop=True).then_inc(s_lg, 1)

            def mix(n):
                e.wait_ge(s_tk, 2 * n + 2)
                e.transpose(tw[n % 2][0:NE, 0:P], rest[:, n, :], ident[:]).then_inc(s_tw, 1)
                e.wait_ge(s_tc, n + 1)
                e.matmul(mx[n % 2][:], wT[:, n % 2, :], ebs[:], start=True, stop=True).then_inc(s_mx, 1)
            for n in range(N + 1):
                if n >= 1:
                    mix(n - 1)
                if n < N:
                    if n >= 2:
                        e.wait_ge(s_z, n - 1)
                    logits(n)

        @block.scalar
        def _(e):
            e.preload_act_table_set("natural_log_exp_and_others")
            e.wait_ge(s_wt, 1)
            e.activation(wrT[:], tw[0][:, 0:C * NE].rearrange("p (c n) -> p c n", n=NE), ACT.Copy)\
                .then_inc(s_wc, 1)

            def rsqrt(k, n):
                e.wait_ge(s_va, k + 1)
                e.activation(rs[:, n, 1:2], rs[:, n, 0:1], ACT.Ln).then_inc(s_ln, 1)
                e.wait_ge(s_ln, k + 1)
                e.activation(rs[:, n, 2:3], rs[:, n, 1:2], ACT.Exp, scale=-0.5).then_inc(s_y0, 1)
            for n in range(N + 1):
                if n < N:
                    rsqrt(first_norm(n), n)
                if n >= 1:
                    m = n - 1
                    e.wait_ge(s_tw, m + 1)
                    e.activation(wT[:, m % 2, :], tw[m % 2][0:NE, 0:P], ACT.Copy).then_inc(s_tc, 1)
                if n < N:
                    e.wait_ge(s_tr, n + 1)
                    e.activation(xT[:, n % 2].rearrange("p c k -> p (c k)"), tr[n % 2][:], ACT.Copy)\
                        .then_inc(s_xT, 1)
                if n >= 1:
                    rsqrt(last_norm(n - 1), n - 1)
                if n < N:
                    e.wait_ge(s_nm, n + 1)
                    e.activation(ex[:, n, :], lg[n % 2][:, 0:NE], ACT.Exp, bias=soft[:, n, 0:1],
                                 accum_out=soft[:, n, 1:2]).then_inc(s_ex, 1)

        @block.vector
        def _(e):
            bns = sms = 0

            def statistics(src, n):
                nonlocal bns
                e.bn_stats(bn[:, n, :], src).then_inc(s_bn, 1)
                e.wait_ge(s_bn, bns + 1)
                e.bn_aggr(mv[:, n, :], bn[:, n, :]).then_inc(s_bn, 1)
                e.wait_ge(s_bn, bns + 2)
                bns += 2
                e.tensor_scalar(rs[:, n, 0:1], mv[:, n, 1:2], 1e-5, None, ALU.add).then_inc(s_va, 1)

            def apply(k, src, dst, n, done):
                e.wait_ge(s_y0, k + 1)
                newton_rsqrt(e, nc, rs[:, n, 0:1], rs[:, n, 2:3], rs[:, n, 3:4], rs[:, n, 4:5],
                             (s_nw, 3 * k)).then_inc(s_nw, 1)
                e.wait_ge(s_nw, 3 * k + 3)
                e.tensor_scalar(dst, src, mv[:, n, 0:1], rs[:, n, 4:5], ALU.subtract, ALU.mult)\
                    .then_inc(done, 1)

            def weights(n):
                nonlocal sms
                e.wait_ge(s_lg, n + 1)
                e.tensor_reduce(soft[:, n, 0:1], lg[n % 2][:, 0:NE], AX.X, ALU.max, negate=True).then_inc(s_nm, 1)
                e.wait_ge(s_ex, n + 1)
                e.reciprocal(soft[:, n, 2:3], soft[:, n, 1:2]).then_inc(s_sm, 1)
                e.wait_ge(s_sm, sms + 1)
                e.tensor_scalar(ex[:, n, :], ex[:, n, :], soft[:, n, 2:3], None, ALU.mult).then_inc(s_sm, 1)
                e.wait_ge(s_sm, sms + 2)
                e.max(top[:, n, :], ex[:, n, :]).then_inc(s_sm, 1)
                e.wait_ge(s_sm, sms + 3)
                e.match_replace(rest[:, n, :], top[:, n, :], ex[:, n, :], 0.0).then_inc(s_sm, 1)
                e.reduce_sum(soft[:, n, 3:4], top[:, n, :], AX.X).then_inc(s_sm, 1)
                e.wait_ge(s_sm, sms + 5)
                sms += 5
                e.tensor_scalar(soft[:, n, 3:4], soft[:, n, 3:4], 1.0, None, ALU.add).then_inc(s_tk, 1)
                e.tensor_tensor(rest[:, n, :], ex[:, n, :], rest[:, n, :], ALU.subtract).then_inc(s_tk, 1)

            def combine(n):
                e.wait_ge(s_mx, n + 1)
                e.scalar_tensor_tensor(z[:, n, :], y[:, n, :], soft[:, n, 3:4], mx[n % 2][:], ALU.mult, ALU.add)\
                    .then_inc(s_z, 1)
                e.wait_ge(s_z, n + 1)
                statistics(z[:, n, :], n)

            for n in range(N + 1):
                if n < N:
                    e.wait_ge(s_y[n], 16)
                    statistics(y[:, n, :], n)
                    apply(first_norm(n), y[:, n, :], y[:, n, :], n, s_x2)
                if n >= 1:
                    combine(n - 1)
                    apply(last_norm(n - 1), z[:, n - 1, :], z[:, n - 1, :], n - 1, s_ou)
                if n < N:
                    weights(n)


def decoder_layer(nc, x, ctx_4096, sWq, sbq, sWk, sbk, sWv, sbv, xWq, xWk, xWv, xWo, xqw, xkw,
                  Wr, rb, eb, out):
    x1 = nc.dram_tensor("x1_scratch", x.shape, F32, kind="Internal").ap()
    x2 = nc.dram_tensor("x2_scratch", x.shape, F32, kind="Internal").ap()
    self_attention(nc, x, sWq, sbq, sWk, sbk, sWv, sbv, x1)
    cross_attention(nc, ctx_4096, xWq, xWk, xWv, xWo, xqw, xkw, x1, x2)
    feed_forward(nc, x2, Wr, rb, eb, out)


_INS = ["x", "ctx_4096", "L0_attn_Wq", "L0_attn_bq", "L0_attn_Wk", "L0_attn_bk", "L0_attn_Wv", "L0_attn_bv",
        "L0_xattn_Wq", "L0_xattn_Wk", "L0_xattn_Wv", "L0_xattn_Wo", "L0_xattn_q_norm_w",
        "L0_xattn_k_norm_w", "L0_ffn_router_weight", "L0_ffn_router_bias", "L0_ffn_expert_bias"]


def kernel(**inputs):
    import numpy as _np
    import concourse.bacc as _bacc
    from concourse import mybir as _mybir
    from concourse.bass_utils import run_bass_kernel_spmd as _run

    nc = _bacc.Bacc("TRN2", target_bir_lowering=False, num_devices=1)
    arrays, args = {}, []
    for name in _INS:
        a = _np.ascontiguousarray(inputs[name])
        arrays[f"in_{name}"] = a
        args.append(nc.dram_tensor(f"in_{name}", a.shape, _mybir.dt.from_np(a.dtype), kind="ExternalInput").ap())
    out = nc.dram_tensor("out_0", inputs["x"].shape, _mybir.dt.float32, kind="ExternalOutput").ap()
    decoder_layer(nc, *args, out)
    r = _run(nc, [arrays], core_ids=[0])
    return r.results[0]["out_0"]
```

```python
from contextlib import ExitStack

import concourse.bass as bass
from concourse import mybir

F32 = mybir.dt.float32
F32R = mybir.dt.float32r
ALU = mybir.AluOpType
ACT = mybir.ActivationFunctionType
AX = mybir.AxisListType
P = 128


def f(ap):
    return ap.bitcast(F32)


def newton_rsqrt(e, nc, x, y0, a, out, step):
    sem, n = step
    e.scalar_tensor_tensor(a, x, -0.5, y0, ALU.mult, ALU.mult).then_inc(sem, 1)
    e.wait_ge(sem, n + 1)
    e.tensor_tensor(a, a, y0, ALU.mult).then_inc(sem, 1)
    e.wait_ge(sem, n + 2)
    return e.scalar_tensor_tensor(out, a, 1.5, y0, ALU.add, ALU.mult)


def self_attention(nc, x, Wq, bq, Wk, bk, Wv, bv, x1):
    B, S, E = x.shape
    D, H = Wq.shape[1:]
    G = Wk.shape[2]
    R = H // G
    C = E // P
    DG = D * G
    NT = 4
    TURNS = B * S // P // NT
    PAIRS = [list(range(t, t + 2)) for t in range(0, NT, 2)]
    DD = 4
    assert TURNS * NT * P == B * S
    xf = x.rearrange("b s e -> (b s) e")
    x1f = x1.rearrange("b s e -> (b s) e")

    with ExitStack() as ctx:
        def sb(name, shape, dt=F32):
            return ctx.enter_context(nc.sbuf_tensor(name, shape, dt))

        def sem(name):
            return ctx.enter_context(nc.semaphore(name))

        w_raw = sb("a_w_raw", [P, C, E])
        w = sb("a_w", [P, C, 3 * DG])
        b_raw = sb("a_b_raw", [1, E])
        bias = sb("a_bias", [1, 3 * DG])
        ones = sb("a_ones", [1, P])
        ident = sb("a_ident", [P, P])
        xt = sb("a_x", [P, NT, E])
        xT = sb("a_xT", [P, NT, C, P])
        qkv = sb("a_qkv", [P, NT, 3 * DG])
        prod = sb("a_prod", [P, NT, D * D * G])
        sc = sb("a_scores", [P, NT, D, D])
        stat = sb("a_stat", [P, NT, 3, D])
        o = sb("a_o", [P, NT, DG])
        bn = sb("a_bn", [P, NT, 6])
        mv = sb("a_mv", [P, NT, 2])
        rs = sb("a_rs", [P, NT, 5])
        tr = [ctx.enter_context(nc.psum_tensor(f"a_tr{i}", [P, C, P], F32)) for i in range(NT)]
        pq = [ctx.enter_context(nc.psum_tensor(f"a_pq{i}", [P, 512], F32)) for i in range(NT)]

        s_w = sem("a_w_loaded")
        s_wr = sem("a_w_reduced")
        s_cst = sem("a_constants")
        s_x = [sem(f"a_x_loaded{i}") for i in range(NT)]
        s_tr = sem("a_transposed")
        s_xT = sem("a_xT_copied")
        s_pq = sem("a_projected")
        s_qkv = sem("a_qkv_copied")
        s_p1 = sem("a_qk_products")
        s_d1 = sem("a_qk_products_of_DVE")
        s_sc = sem("a_scores_summed")
        s_mx = sem("a_row_max")
        s_sh = sem("a_scores_shifted")
        s_ex = sem("a_exponentials")
        s_su = sem("a_row_sums")
        s_ri = sem("a_row_reciprocals")
        s_pr = sem("a_probabilities")
        s_p2 = sem("a_pv_products")
        s_d2 = sem("a_pv_products_of_DVE")
        s_o = sem("a_outputs_summed")
        s_h = sem("a_residual_added")
        s_bn = sem("a_bn_steps")
        s_go = sem("a_statistics_seen")
        s_va = sem("a_variance")
        s_ln = sem("a_log_variance")
        s_y0 = sem("a_rsqrt_estimate")
        s_nw = sem("a_newton_steps")
        s_x1 = sem("a_normalised")
        s_st = [sem(f"a_x1_stored{i}") for i in range(NT)]

        block = ctx.enter_context(nc.Block())

        @block.sync
        def _(e):
            with e.Fori(0, TURNS) as i:
                for t in range(NT):
                    e.wait_ge(s_st[t], 16 * i + 16)
                    e.dma_start(xt[:, t, :], xf[bass.ds((NT * i + t) * P, P), :]).then_inc(s_x[t], 16)
                for t in range(NT):
                    e.wait_ge(s_x1, NT * i + t + 1)
                    e.dma_start(x1f[bass.ds((NT * i + t) * P, P), :], xt[:, t, :]).then_inc(s_st[t], 16)
            for t in range(NT):
                e.wait_ge(s_st[t], 16 * TURNS + 16)

        def qk_products(e, t, ds):
            n = ds.stop - ds.start
            q = qkv[:, t, 0:DG].rearrange("p (d g) -> p d g", g=G)[:, ds]
            k = qkv[:, t, DG:2 * DG].rearrange("p (e g) -> p e g", g=G)
            return e.tensor_tensor(prod[:, t, :].rearrange("p (d e g) -> p d e g", d=D, e=D)[:, ds],
                                   q.unsqueeze(2).to_broadcast([P, n, D, G]),
                                   k.unsqueeze(1).to_broadcast([P, n, D, G]), ALU.mult)

        def pv_products(e, t, ds):
            n = ds.stop - ds.start
            v = qkv[:, t, 2 * DG:].rearrange("p (e g) -> p g e", g=G)
            return e.tensor_tensor(prod[:, t, :].rearrange("p (d g e) -> p d g e", d=D, g=G)[:, ds],
                                   sc[:, t, ds].unsqueeze(2).to_broadcast([P, n, G, D]),
                                   v.unsqueeze(1).to_broadcast([P, n, G, D]), ALU.mult)

        @block.gpsimd
        def _(e):
            for t in range(NT):
                e.sem_inc(s_st[t], 16)
            e.memset(ones[:], 1.0).then_inc(s_cst, 1)
            e.memset(ident[:], 0.0).then_inc(s_cst, 1)
            e.wait_ge(s_cst, 2)
            e.affine_select(out=ident[:], in_=ident[:], compare_op=ALU.not_equal, fill=1.0, base=0,
                            pattern=[[-1, P]], channel_multiplier=1).then_inc(s_cst, 1)
            with e.Fori(0, TURNS) as i:
                for t in range(NT):
                    e.wait_ge(s_qkv, NT * i + t + 1)
                    qk_products(e, t, slice(DD, D)).then_inc(s_p1, 1)
                for t in range(NT):
                    e.wait_ge(s_pr, NT * i + t + 1)
                    pv_products(e, t, slice(DD, D)).then_inc(s_p2, 1)

        @block.tensor
        def _(e):
            e.wait_ge(s_cst, 3)
            e.wait_ge(s_wr, 2)
            e.wait_ge(s_w, 96)
            with e.Fori(0, TURNS) as i:
                for t in range(NT):
                    e.wait_ge(s_x[t], 16 * i + 16)
                    for c in range(C):
                        ins = e.transpose(tr[t][:, c, :], xt[:, t, c * P:(c + 1) * P], ident[:])
                    ins.then_inc(s_tr, 1)
                for t in range(NT):
                    e.wait_ge(s_xT, NT * i + t + 1)
                    for c in range(C):
                        e.matmul(pq[t][:, 0:3 * DG], xT[:, t, c, :], w[:, c, :], start=(c == 0), stop=False)
                    e.matmul(pq[t][:, 0:3 * DG], ones[:], bias[:], start=False, stop=True).then_inc(s_pq, 1)

        @block.scalar
        def _(e):
            e.dma_start(w_raw[:], Wq.rearrange("(c p) d h -> p c (d h)", p=P)).then_inc(s_w, 16)
            e.dma_start(w[:, :, DG:2 * DG], Wk.rearrange("(c p) d g -> p c (d g)", p=P)).then_inc(s_w, 16)
            e.dma_start(w[:, :, 2 * DG:], Wv.rearrange("(c p) d g -> p c (d g)", p=P)).then_inc(s_w, 16)
            e.dma_start(b_raw[:], bq.rearrange("(o d) h -> o (d h)", o=1)).then_inc(s_w, 16)
            e.dma_start(bias[:, DG:2 * DG], bk.rearrange("(o d) g -> o (d g)", o=1)).then_inc(s_w, 16)
            e.dma_start(bias[:, 2 * DG:], bv.rearrange("(o d) g -> o (d g)", o=1)).then_inc(s_w, 16)
            e.preload_act_table_set("natural_log_exp_and_others")

            def project(i, t):
                n = NT * i + t + 1
                e.wait_ge(s_pq, n)
                e.activation(qkv[:, t, :], pq[t][:, 0:3 * DG], ACT.Copy).then_inc(s_qkv, 1)

            with e.Fori(0, TURNS) as i:
                for t in range(NT):
                    e.wait_ge(s_tr, NT * i + t + 1)
                    e.activation(xT[:, t], tr[t][:], ACT.Copy).then_inc(s_xT, 1)
                for t in range(NT):
                    project(i, t)
                for t in range(NT):
                    e.wait_ge(s_sh, NT * i + t + 1)
                    e.activation(sc[:, t], sc[:, t], ACT.Exp, scale=float(D) ** -0.5).then_inc(s_ex, 1)
                for t in range(NT):
                    n = NT * i + t + 1
                    e.wait_ge(s_va, n)
                    e.activation(rs[:, t, 1:2], rs[:, t, 0:1], ACT.Ln).then_inc(s_ln, 1)
                    e.wait_ge(s_ln, n)
                    e.activation(rs[:, t, 2:3], rs[:, t, 1:2], ACT.Exp, scale=-0.5).then_inc(s_y0, 1)

        @block.vector
        def _(e):
            e.wait_ge(s_w, 96)
            e.reduce_sum(w[:, :, 0:DG], w_raw[:].rearrange("p c (n r) -> p c n r", r=R), AX.X).then_inc(s_wr, 1)
            e.reduce_sum(bias[:, 0:DG], b_raw[:].rearrange("p (n r) -> p n r", r=R), AX.X).then_inc(s_wr, 1)
            with e.Fori(0, TURNS) as i:
                def products(t):
                    e.wait_ge(s_qkv, NT * i + t + 1)
                    qk_products(e, t, slice(0, DD)).then_inc(s_d1, 1)

                def scores(t):
                    n = NT * i + t + 1
                    e.wait_ge(s_p1, n)
                    e.wait_ge(s_d1, n)
                    e.reduce_sum(sc[:, t], prod[:, t, :].rearrange("p (d e g) -> p d e g", d=D, e=D), AX.X)\
                        .then_inc(s_sc, 1)
                    e.wait_ge(s_sc, n)
                    e.reduce_max(stat[:, t, 0, :], sc[:, t], AX.X).then_inc(s_mx, 1)
                    e.wait_ge(s_mx, n)
                    e.tensor_tensor(sc[:, t], sc[:, t], stat[:, t, 0, :].unsqueeze(2).to_broadcast([P, D, D]),
                                    ALU.subtract).then_inc(s_sh, 1)

                def normalise(t):
                    n = NT * i + t + 1
                    e.wait_ge(s_ex, n)
                    e.reduce_sum(stat[:, t, 1, :], sc[:, t], AX.X).then_inc(s_su, 1)
                    e.wait_ge(s_su, n)
                    e.reciprocal(stat[:, t, 2, :], stat[:, t, 1, :]).then_inc(s_ri, 1)
                    e.wait_ge(s_ri, n)
                    e.tensor_tensor(sc[:, t], sc[:, t], stat[:, t, 2, :].unsqueeze(2).to_broadcast([P, D, D]),
                                    ALU.mult).then_inc(s_pr, 1)
                    e.wait_ge(s_pr, n)
                    pv_products(e, t, slice(0, DD)).then_inc(s_d2, 1)

                def residual(t):
                    n = NT * i + t + 1
                    e.wait_ge(s_p2, n)
                    e.wait_ge(s_d2, n)
                    e.reduce_sum(o[:, t, :], prod[:, t, :].rearrange("p (n e) -> p n e", e=D), AX.X)\
                        .then_inc(s_o, 1)
                    e.wait_ge(s_o, n)
                    h = xt[:, t, :].rearrange("p (n r) -> p n r", r=R)
                    e.tensor_tensor(h, h, o[:, t, :].unsqueeze(2).to_broadcast([P, DG, R]), ALU.add)\
                        .then_inc(s_h, 1)
                    e.wait_ge(s_h, n)
                    e.bn_stats(bn[:, t, :], xt[:, t, :]).then_inc(s_bn, 1)
                    e.wait_ge(s_bn, 2 * n - 1)
                    e.sem_inc(s_go, 1)
                    e.bn_aggr(mv[:, t, :], bn[:, t, :]).then_inc(s_bn, 1)
                    e.wait_ge(s_bn, 2 * n)
                    e.tensor_scalar(rs[:, t, 0:1], mv[:, t, 1:2], 1e-5, None, ALU.add).then_inc(s_va, 1)

                def layernorm(t):
                    n = NT * i + t + 1
                    e.wait_ge(s_y0, n)
                    newton_rsqrt(e, nc, rs[:, t, 0:1], rs[:, t, 2:3], rs[:, t, 3:4], rs[:, t, 4:5],
                                 (s_nw, 3 * n - 3)).then_inc(s_nw, 1)
                    e.wait_ge(s_nw, 3 * n)
                    e.tensor_scalar(xt[:, t, :], xt[:, t, :], mv[:, t, 0:1], rs[:, t, 4:5],
                                    ALU.subtract, ALU.mult).then_inc(s_x1, 1)

                for pair in PAIRS:
                    for step in (products, scores, normalise):
                        for t in pair:
                            step(t)
                for step in (residual, layernorm):
                    for t in range(NT):
                        step(t)


START, MID, TURN, LAST = "start", "mid", "turn", "last"


def cross_attention(nc, ctx_in, Wq, Wk, Wv, Wo, qw, kw, x1, y_out):
    B, L, E = ctx_in.shape
    S = x1.shape[1]
    HD = P
    KVH = Wk.shape[1] // HD
    GR = Wq.shape[1] // HD // KVH
    C = E // P
    TPB = S // P
    NK = L + S
    NJ = -(-NK // P)
    TAIL = NK - (NJ - 1) * P
    NKP = NJ * P
    NQ = GR * TPB
    CH = [(c * 512, min(512, NK - c * 512)) for c in range(-(-NK // 512))]
    CH = [(o, n + n % 2) for o, n in CH]
    SETS = [list(range(4 * s, min(4 * s + 4, NJ))) for s in range(-(-NJ // 4))]
    assert TPB == 2 and GR == 4 and C == 4 and len(CH) == 4 and len(SETS) == 4 and NQ == 8
    SPLIT = 512
    H1 = 8
    EPS = 1e-6

    X_IN_STEP = {i: [n for n in range(NJ) if n * (NQ - 1) // NJ + 1 == i] for i in range(1, NQ)}

    def ring_order(kind):
        order = []
        if kind == START:
            order += [("X", n) for n in range(NJ)]
        else:
            for i in range(1, NQ):
                order += [("T", i - 1, s) for s in range(4)]
                if kind == TURN:
                    order += [("X", n) for n in X_IN_STEP[i]]
            order += [("T", NQ - 1, s) for s in range(4)]
        if kind == LAST:
            return order + [("O", 0), ("O", 1)]
        order += [("KT", 0), ("KT", 1), ("Q", 0), ("KT", 2), ("QT", 0), ("Q", 1), ("KT", 3), ("O", 0),
                  ("QT", 1), ("O", 1)]
        return [x for x in order if kind != START or x[0] != "O"]

    RING = {k: ring_order(k) for k in (START, MID, TURN, LAST)}
    HI = {k: [x for x in v if x[0] in ("X", "T", "KT", "QT")] for k, v in RING.items()}
    assert len(RING[MID]) % 3 == 0 and len(RING[TURN]) % 3 == 0

    class Unit:

        def __init__(self, kind, b, h):
            self.kind, self.b, self.h = kind, b, h
            self.u = -1 if kind == START else b * KVH + h

            def before(table):
                if kind == START:
                    return 0
                per_batch = (KVH - 1) * len(table[MID]) + len(table[TURN])
                return len(table[START]) + b * per_batch + h * len(table[MID])
            self.ring0, self.hi0 = before(RING), before(HI)

        def ring(self, *label):
            return self.ring0 + RING[self.kind].index(label) + 1

        def hi(self, *label):
            return self.hi0 + HI[self.kind].index(label) + 1

        def bank(self, *label):
            first = 0 if self.kind == START else len(RING[START])
            return (first + RING[self.kind].index(label)) % 3

        def has_next(self):
            return self.kind != LAST

    def units(e, body):
        body(Unit(START, 0, 0))
        with e.Fori(0, B - 1) as b:
            with e.Fori(0, KVH - 1) as h:
                body(Unit(MID, b, h))
            body(Unit(TURN, b, KVH - 1))
        with e.Fori(0, KVH - 1) as h:
            body(Unit(MID, B - 1, h))
        body(Unit(LAST, B - 1, KVH - 1))

    with ExitStack() as ctx:
        def sb(name, shape, dt=F32):
            return ctx.enter_context(nc.sbuf_tensor(name, shape, dt))

        def sem(name):
            return ctx.enter_context(nc.semaphore(name))

        def pair(name, shape):
            return sb(name + "_hi", shape, F32R), sb(name + "_lo", shape, F32R)

        kvT_hi, kvT_lo = pair("kvT", [P, C, NKP])
        KT_hi, KT_lo = pair("KT", [P, NKP])
        V_hi, V_lo = pair("V", [P, NJ, HD])
        PT_hi, PT_lo = pair("PT", [P, NJ, TPB * P])
        QT_hi, QT_lo = pair("QT", [P, GR, TPB * P])
        OT_hi, OT_lo = pair("OT", [P, GR, TPB * P])
        Wkv_hi, Wkv_lo = pair("Wkv", [P, C, 2 * HD])
        Wq_hi, Wq_lo = pair("Wq", [P, C, GR * HD])
        Wo_hi, Wo_lo = pair("Wo", [P, GR, E])
        stage = sb("w_stage", [P, 1024])
        prob = sb("prob", [P, 2, NKP])
        nat = sb("nat", [P, 2, 4, HD])
        y = sb("y", [P, TPB, E])
        ident = sb("ident", [P, P])
        one = sb("one", [P, 1])
        qkw = sb("qkw", [P, 3])
        pm = sb("pm", [P, 2, 3])
        nm = sb("nm", [P, 2])
        rsum = sb("rsum", [P, 2, 2])
        rinv = sb("rinv", [P, 2, 2])
        nrm = sb("nrm", [P, 6, 4])

        S_ps = ctx.enter_context(nc.psum_tensor("S_ps", [P, 4 * 512], F32))
        ring_ps = [ctx.enter_context(nc.psum_tensor(f"ring{i}", [P, 512], F32)) for i in range(3)]
        OT_ps = ctx.enter_context(nc.psum_tensor("OT_ps", [P, 512], F32))
        KV_ps = S_ps[:].rearrange("p (a n) -> p a n", n=2 * HD)

        s_id = sem("identity")
        s_pad = sem("pads_zeroed")
        s_qkw = sem("norm_weights_loaded")
        s_w = sem("norm_weight_ready")
        s_wd = sem("weights_loaded")
        s_ws = sem("weights_split")
        s_xd = [sem(f"key_rows_loaded{i}") for i in range(2)]
        s_yd = sem("y_moved")
        s_full = sem("ring_full")
        s_free = sem("ring_free")
        s_hi = sem("ring_hi_copied")
        s_sc = sem("scores_full")
        s_max = sem("chunk_max")
        s_nm = sem("negated_max")
        s_exp = sem("exponentials")
        s_rs = sem("row_sum")
        s_ri = sem("row_reciprocal")
        s_pn = sem("left_probabilities_normed")
        s_pa = sem("right_probabilities_normed")
        s_of = sem("OT_full")
        s_oh = sem("OT_hi_copied")
        s_ol = sem("OT_lo_copied")
        s_kv = sem("KV_full")
        s_sq = sem("squares")
        s_ss = sem("sum_of_squares")
        s_ms = sem("mean_square")
        s_ln = sem("log_mean_square")
        s_y0 = sem("rsqrt_estimate")
        s_nw = sem("newton_steps")
        s_nat = sem("rows_normed")
        s_vh = sem("V_hi_copied")
        s_vl = sem("V_lo_copied")

        block = ctx.enter_context(nc.Block())

        def target(label, bank):
            ps = ring_ps[bank][:]
            if label[0] == "T":
                _, i, s = label
                n, q = len(SETS[s]), (i % TPB) * P
                return (ps[:, 0:n * P].rearrange("p (j q) -> p j q", q=P),
                        PT_hi[:, 4 * s:4 * s + n, q:q + P], PT_lo[:, 4 * s:4 * s + n, q:q + P])
            if label[0] == "KT":
                n = len(SETS[label[1]]) * P
                at = label[1] * 512
                return ps[:, 0:n], KT_hi[:, at:at + n], KT_lo[:, at:at + n]
            if label[0] == "QT":
                q = label[1] * P
                return (ps.rearrange("p (h q) -> p h q", q=P), QT_hi[:, :, q:q + P], QT_lo[:, :, q:q + P])
            n = label[1]
            rows = P if n < NJ - 1 else TAIL
            return (ps.rearrange("p (c k) -> p c k", k=P)[:, :, 0:rows],
                    kvT_hi[:, :, n * P:n * P + rows], kvT_lo[:, :, n * P:n * P + rows])

        JOBS = [("KV", 0), ("KV", 1), ("KV", 2), ("Q", 0), ("KV", 3), ("Q", 1)]
        OUT = {("KV", g): ("KT", g) for g in range(4)} | {("Q", t): ("QT", t) for t in range(TPB)}

        def job_no(U, job):
            return 6 * (U.u + 1) + JOBS.index(job) + 1

        def job_source(U, job):
            if job[0] == "Q":
                return ring_ps[U.bank(*job)][:].rearrange("p (h d) -> p h d", d=HD)
            g = job[1]
            a = 4 * (g % 2)
            return KV_ps[:, a:a + len(SETS[g]), 0:HD]

        def v_source(g):
            a = 4 * (g % 2)
            return KV_ps[:, a:a + len(SETS[g]), HD:2 * HD]

        def weights_split(U, n):
            return 2 * n if U.kind == START else 2 * (3 + 5 * U.u + n)

        @block.sync
        def _(e):
            e.dma_start(qkw[:, 0:1], qw.rearrange("(p o) -> p o", o=1)).then_inc(s_qkw, 16)
            e.dma_start(qkw[:, 1:2], kw.rearrange("(p o) -> p o", o=1)).then_inc(s_qkw, 16)
            e.dma_start(y[:], x1[0].rearrange("(t p) e -> p t e", p=P)).then_inc(s_yd, 16)
            wk = Wk.rearrange("(c p) n -> p c n", p=P)
            wv = Wv.rearrange("(c p) n -> p c n", p=P)
            wq = Wq.rearrange("(c p) n -> p c n", p=P)
            wo = Wo.rearrange("(g p) n -> p g n", p=P)

            def body(U):
                job = 0

                def free(n):
                    if not (U.kind == START and n == 0):
                        e.wait_ge(s_ws, weights_split(U, n))
                if U.has_next():
                    h = 0 if U.kind in (START, TURN) else U.h + 1
                    st = stage[:].rearrange("p (c n) -> p c n", c=C)
                    free(0)
                    e.dma_start(st[:, :, 0:HD], wk[:, :, bass.ts(h, HD)]).then_inc(s_wd, 16)
                    e.dma_start(st[:, :, HD:2 * HD], wv[:, :, bass.ts(h, HD)]).then_inc(s_wd, 16)
                    for a in range(2):
                        free(1 + a)
                        e.dma_start(stage[:].rearrange("p (c n) -> p c n", c=2),
                                    wq[:, 2 * a:2 * a + 2, bass.ts(h, GR * HD)]).then_inc(s_wd, 16)
                    job = 3
                if U.kind != START:
                    for a in range(2):
                        free(job + a)
                        e.dma_start(stage[:].rearrange("p (c n) -> p c n", c=2),
                                    wo[:, bass.ds(U.h * GR + 2 * a, 2), :]).then_inc(s_wd, 16)
                if U.kind in (TURN, LAST):
                    e.wait_ge(s_free, U.ring("O", 1))
                    e.dma_start(y_out[bass.ds(U.b, 1)].rearrange("o (t p) e -> p (o t) e", p=P), y[:])\
                        .then_inc(s_yd, 16)
                    e.wait_ge(s_yd, 32 * U.b + 32)
                if U.kind == TURN:
                    e.dma_start(y[:], x1[bass.ds(U.b + 1, 1)].rearrange("o (t p) e -> p (o t) e", p=P))\
                        .then_inc(s_yd, 16)
            units(e, body)

        @block.gpsimd
        def _(e):
            e.sem_inc(s_ol, 1)
            e.memset(ident[:], 0.0).then_inc(s_id, 1)
            e.wait_ge(s_id, 1)
            e.affine_select(out=ident[:], in_=ident[:], compare_op=ALU.not_equal, fill=1.0, base=0,
                            pattern=[[-1, P]], channel_multiplier=1).then_inc(s_id, 1)
            e.memset(one[:], 1.0).then_inc(s_id, 1)
            e.memset(f(kvT_hi[:, :, NK:NKP]), 0.0).then_inc(s_pad, 1)
            e.memset(f(kvT_lo[:, :, NK:NKP]), 0.0).then_inc(s_pad, 1)
            e.memset(prob[:, :, NK:NKP], 0.0).then_inc(s_pad, 1)

            def body(U):
                dmas = 0 if U.kind == START else 16 * (4 + 6 * U.u)
                n = 0
                if U.kind == START:
                    e.wait_ge(s_id, 3)
                else:
                    e.wait_ge(s_full, U.ring0)

                def split(src, hi, lo, loads):
                    nonlocal dmas, n
                    dmas = dmas + 16 * loads
                    e.wait_ge(s_wd, dmas)
                    e.tensor_tensor(hi, src, one[:].unsqueeze(2).to_broadcast(list(src.shape)), ALU.mult).then_inc(s_ws, 1)
                    e.wait_ge(s_ws, weights_split(U, n) + 1)
                    e.tensor_tensor(lo, src, f(hi), ALU.subtract).then_inc(s_ws, 1)
                    n += 1
                if U.has_next():
                    split(stage[:].rearrange("p (c n) -> p c n", c=C), Wkv_hi[:], Wkv_lo[:], 2)
                    for a in range(2):
                        split(stage[:].rearrange("p (c n) -> p c n", c=2),
                              Wq_hi[:, 2 * a:2 * a + 2, :], Wq_lo[:, 2 * a:2 * a + 2, :], 1)
                if U.kind != START:
                    for a in range(2):
                        split(stage[:].rearrange("p (c n) -> p c n", c=2),
                              Wo_hi[:, 2 * a:2 * a + 2, :], Wo_lo[:, 2 * a:2 * a + 2, :], 1)
            units(e, body)

        @block.tensor
        def _(e):
            e.wait_ge(s_id, 2)
            e.wait_ge(s_pad, 3)

            def three(out, l_hi, l_lo, r_hi, r_lo, first, last):
                e.matmul(out, l_hi, r_hi, start=first, stop=False)
                e.matmul(out, l_hi, r_lo, start=False, stop=False)
                return e.matmul(out, l_lo, r_hi, start=False, stop=last)

            def body(U):
                u = U.u

                def take(*label):
                    if not (U.kind == START and RING[START].index(label) < 3):
                        e.wait_ge(s_free, U.ring(*label) - 3)
                    return ring_ps[U.bank(*label)][:]

                def rows_in(n):
                    before = 0 if U.kind == START else (U.b + 1) * len(range(n % 2, NJ, 2))
                    e.wait_ge(s_xd[n % 2], 16 * (before + n // 2 + 1))
                    ps = take("X", n)
                    rows = P if n < NJ - 1 else TAIL
                    for c in range(C):
                        ins = e.transpose(ps[:, c * P:c * P + rows], nat[0:rows, n % 2, c, :],
                                          ident[0:rows, 0:rows])
                    ins.then_inc(s_full, 1)

                def scores(i, c):
                    at, n = CH[c]
                    g, q = i % NQ // TPB, (i % TPB) * P
                    if i == NQ:
                        if c == 0:
                            e.wait_ge(s_free, U.ring("QT", 0))
                            e.wait_ge(s_nat, job_no(U, ("KV", 2)))
                            e.wait_ge(s_vl, 4 * (u + 1) + 3)
                        elif c == 2:
                            e.wait_ge(s_free, U.ring("KT", 2))
                            e.wait_ge(s_nat, job_no(U, ("KV", 3)))
                            e.wait_ge(s_vl, 4 * (u + 1) + 4)
                        elif c == 3:
                            e.wait_ge(s_free, U.ring("KT", 3))
                    elif c <= 1:
                        e.wait_ge(s_exp, 2 * (NQ * u + i - 1) + 1 + c)
                    three(S_ps[:, c * 512:c * 512 + n], QT_hi[:, g, q:q + P], QT_lo[:, g, q:q + P],
                          KT_hi[:, at:at + n], KT_lo[:, at:at + n], True, True).then_inc(s_sc, 1)

                def turn(i, s):
                    if s == 0:
                        e.wait_ge(s_pn, NQ * u + i + 1)
                    if s == SPLIT // 512:
                        e.wait_ge(s_pa, NQ * u + i + 1)
                    ps = take("T", i, s)
                    for k, j in enumerate(SETS[s]):
                        ins = e.transpose(ps[:, k * P:(k + 1) * P], prob[:, i % 2, j * P:(j + 1) * P], ident[:])
                    ins.then_inc(s_full, 1)

                def pv(g, js):
                    for j in js:
                        if j == 0:
                            e.wait_ge(s_ol, GR * u + g + 1)
                        if j % 4 == 0:
                            e.wait_ge(s_free, U.ring("T", TPB * g + 1, j // 4))
                        ins = three(OT_ps[:, 0:TPB * P], V_hi[:, j, :], V_lo[:, j, :],
                                    PT_hi[:, j, :], PT_lo[:, j, :], j == 0, j == NJ - 1)
                    if js[-1] == NJ - 1:
                        ins.then_inc(s_of, 1)

                def kv(g, ks):
                    if ks[0] == SETS[g][0]:
                        if g == 0:
                            e.wait_ge(s_ws, weights_split(U, 1))
                        if g < 2:
                            if U.kind == START:
                                e.wait_ge(s_free, NJ)
                            else:
                                e.wait_ge(s_exp, 2 * NQ * (u + 1))
                                if U.kind == TURN:
                                    e.wait_ge(s_free, U.ring("X", NJ - 1))
                        else:
                            e.wait_ge(s_nat, job_no(U, ("KV", g - 2)))
                            e.wait_ge(s_vl, 4 * (u + 1) + g - 1)
                    for j in ks:
                        out = KV_ps[:, 4 * (g % 2) + j % 4, :]
                        for c in range(C):
                            ins = three(out, kvT_hi[:, c, j * P:(j + 1) * P], kvT_lo[:, c, j * P:(j + 1) * P],
                                        Wkv_hi[:, c, :], Wkv_lo[:, c, :], c == 0, c == C - 1)
                    if ks[-1] == SETS[g][-1]:
                        ins.then_inc(s_kv, 1)

                def queries(t):
                    if t == 0:
                        e.wait_ge(s_ws, weights_split(U, 3))
                    ps = take("Q", t)
                    for c in range(C):
                        ins = three(ps, kvT_hi[:, c, t * P:(t + 1) * P], kvT_lo[:, c, t * P:(t + 1) * P],
                                    Wq_hi[:, c, :], Wq_lo[:, c, :], c == 0, c == C - 1)
                    ins.then_inc(s_full, 1)

                def rows_out(job):
                    e.wait_ge(s_nat, job_no(U, job))
                    ps = take(*OUT[job])
                    n = GR if job[0] == "Q" else len(SETS[job[1]])
                    for k in range(n):
                        ins = e.transpose(ps[:, k * P:(k + 1) * P], nat[:, JOBS.index(job) % 2, k, :], ident[:])
                    ins.then_inc(s_full, 1)

                def output(t, gs):
                    if (t, gs[0]) == (0, 0):
                        e.wait_ge(s_ws, weights_split(U, 5 if U.has_next() else 2))
                        e.wait_ge(s_ol, GR * (u + 1) + 1)
                    ps = take("O", t) if gs[0] == 0 else ring_ps[U.bank("O", t)][:]
                    for g in gs:
                        ins = three(ps, OT_hi[:, g, t * P:(t + 1) * P], OT_lo[:, g, t * P:(t + 1) * P],
                                    Wo_hi[:, g, :], Wo_lo[:, g, :], g == 0, g == GR - 1)
                    if gs[-1] == GR - 1:
                        ins.then_inc(s_full, 1)

                first_half, rest = list(range(H1)), list(range(H1, NJ))
                if U.kind == START:
                    for n in range(NJ):
                        rows_in(n)
                    for g in range(2):
                        kv(g, SETS[g])
                        rows_out(("KV", g))
                else:
                    for i in range(1, NQ):
                        g = i // TPB - 1
                        scores(i, 0)
                        scores(i, 1)
                        turn(i - 1, 0)
                        scores(i, 2)
                        turn(i - 1, 1)
                        scores(i, 3)
                        if i % 2 == 0:
                            turn(i - 1, 2)
                            turn(i - 1, 3)
                            pv(g, first_half)
                        else:
                            if g >= 0:
                                pv(g, rest[:4])
                            turn(i - 1, 2)
                            if g >= 0:
                                pv(g, rest[4:])
                            turn(i - 1, 3)
                        if U.kind == TURN:
                            for n in X_IN_STEP[i]:
                                rows_in(n)
                    i = NQ - 1
                    if U.has_next():
                        kv(0, SETS[0][0:2])
                    turn(i, 0)
                    turn(i, 1)
                    if U.has_next():
                        kv(0, SETS[0][2:4])
                    turn(i, 2)
                    turn(i, 3)
                    if U.has_next():
                        kv(1, SETS[1][0:2])
                    pv(GR - 1, first_half + rest)
                    if U.has_next():
                        kv(1, SETS[1][2:4])
                        rows_out(("KV", 0))
                if U.has_next():
                    kv(2, SETS[2])
                    if U.kind != START:
                        rows_out(("KV", 1))
                    queries(0)
                    kv(3, SETS[3])
                    rows_out(("KV", 2))
                    rows_out(("Q", 0))
                    queries(1)
                    scores(NQ, 0)
                    scores(NQ, 1)
                heads = list(range(GR))
                if U.kind != START:
                    output(0, heads[:2])
                if U.has_next():
                    rows_out(("KV", 3))
                if U.kind != START:
                    output(0, heads[2:])
                if U.has_next():
                    scores(NQ, 2)
                    rows_out(("Q", 1))
                    scores(NQ, 3)
                if U.kind != START:
                    output(1, heads)
                if U.has_next():
                    e.wait_ge(s_free, U.ring("QT", 1))
            units(e, body)

        @block.scalar
        def _(e):
            e.preload_act_table_set("natural_log_exp_and_others")
            e.wait_ge(s_pad, 3)

            def body(U):
                u = U.u

                def load_rows(n):
                    rows = P if n < NJ - 1 else TAIL
                    b = 0 if U.kind == START else U.b + 1
                    if n < TPB:
                        src = x1[bass.ds(b, 1), n * P:n * P + rows, :]
                    else:
                        src = ctx_in[bass.ds(b, 1), (n - TPB) * P:(n - TPB) * P + rows, :]
                    if n >= 2:
                        e.wait_ge(s_full, U.ring("X", n - 2))
                    elif U.kind != START:
                        e.wait_ge(s_full, U.ring0)
                    e.dma_start(nat[0:rows, n % 2].rearrange("p c d -> p (c d)"),
                                src.rearrange("o p e -> (o p) e")).then_inc(s_xd[n % 2], 16)

                def hi(*label):
                    ps, dst, _ = target(label, U.bank(*label))
                    e.wait_ge(s_full, U.ring(*label))
                    if label[0] == "QT":
                        e.activation(dst, ps, ACT.Copy, scale=qkw[:, 2:3]).then_inc(s_hi, 1)
                    else:
                        e.activation(dst, ps, ACT.Copy).then_inc(s_hi, 1)
                    if label[0] == "X" and label[1] + 2 < NJ:
                        load_rows(label[1] + 2)

                def norm(i):
                    e.wait_ge(s_ri, NQ * u + i + 1)
                    p = prob[:, i % 2, SPLIT:NK]
                    e.activation(p, p, ACT.Copy, scale=rinv[:, i % 2, 1:2]).then_inc(s_pa, 1)

                def exps(i, half):
                    at, to = ((0, 512), (512, NK))[half]
                    if half == 0:
                        e.wait_ge(s_nm, NQ * u + i + 1)
                    if half == 0 and i != 1 and U.kind != START:
                        e.wait_ge(s_full, U.ring("T", i - 2, 3))
                    e.activation(prob[:, i % 2, at:to], S_ps[:, at:to], ACT.Exp, bias=nm[:, i % 2:i % 2 + 1],
                                 accum_out=rsum[:, i % 2, half:half + 1]).then_inc(s_exp, 1)

                def out_hi(g):
                    e.wait_ge(s_of, GR * u + g + 1)
                    e.activation(OT_hi[:, g, :], OT_ps[:, 0:TPB * P], ACT.Copy).then_inc(s_oh, 1)

                def squares(job):
                    no = JOBS.index(job)
                    n = job_no(U, job)
                    if job[0] == "Q":
                        e.wait_ge(s_full, U.ring(*job))
                    else:
                        e.wait_ge(s_kv, 4 * (u + 1) + job[1] + 1)
                    if no >= 2:
                        e.wait_ge(s_full, U.ring(*OUT[JOBS[no - 2]]))
                    src = job_source(U, job)
                    k = src.shape[1]
                    e.activation(nat[:, no % 2, 0:k, :], src, ACT.Square).then_inc(s_sq, 1)
                    if job[0] == "KV" and job[1] > 0:
                        v_hi(job[1])
                    e.wait_ge(s_ms, n)
                    e.activation(nrm[:, 2, 0:k], nrm[:, 1, 0:k], ACT.Ln).then_inc(s_ln, 1)
                    e.wait_ge(s_ln, n)
                    e.activation(nrm[:, 3, 0:k], nrm[:, 2, 0:k], ACT.Exp, scale=-0.5).then_inc(s_y0, 1)

                def v_hi(g):
                    e.wait_ge(s_kv, 4 * (u + 1) + g + 1)
                    if g == 0:
                        e.wait_ge(s_nat, job_no(U, ("KV", 0)))
                    if g < 2 and U.kind != START:
                        e.wait_ge(s_of, GR * (u + 1))
                    e.activation(V_hi[:, 4 * g:4 * g + len(SETS[g]), :], v_source(g), ACT.Copy).then_inc(s_vh, 1)

                if U.kind == START:
                    load_rows(0)
                    load_rows(1)
                    for n in range(NJ):
                        hi("X", n)
                    e.wait_ge(s_w, 1)
                    squares(("KV", 0))
                    v_hi(0)
                    hi("KT", 0)
                    squares(("KV", 1))
                    hi("KT", 1)
                else:
                    if U.kind == TURN:
                        load_rows(0)
                        load_rows(1)
                    for i in range(1, NQ):
                        hi("T", i - 1, 0)
                        hi("T", i - 1, 1)
                        if i % 2 == 0:
                            hi("T", i - 1, 2)
                            exps(i, 0)
                            exps(i, 1)
                            hi("T", i - 1, 3)
                            norm(i)
                        else:
                            exps(i, 0)
                            exps(i, 1)
                            hi("T", i - 1, 2)
                            hi("T", i - 1, 3)
                            norm(i)
                        if i % 2 and i >= 3:
                            out_hi((i - 3) // 2)
                        if U.kind == TURN:
                            for n in X_IN_STEP[i]:
                                hi("X", n)
                    i = NQ - 1
                    hi("T", i, 0)
                    hi("T", i, 1)
                    if U.has_next():
                        squares(("KV", 0))
                    hi("T", i, 2)
                    hi("T", i, 3)
                    out_hi(GR - 1)
                    if U.has_next():
                        v_hi(0)
                        squares(("KV", 1))
                        hi("KT", 0)
                if U.has_next():
                    squares(("KV", 2))
                    if U.kind != START:
                        hi("KT", 1)
                    squares(("Q", 0))
                    hi("KT", 2)
                    hi("QT", 0)
                    squares(("KV", 3))
                    squares(("Q", 1))
                    hi("KT", 3)
                    hi("QT", 1)
                    exps(NQ, 0)
                    exps(NQ, 1)
                    norm(NQ)
            units(e, body)

        @block.vector
        def _(e):
            e.wait_ge(s_qkw, 32)
            e.scalar_tensor_tensor(qkw[:, 2:3], qkw[:, 0:1], float(HD) ** -0.5, qkw[:, 1:2],
                                   ALU.mult, ALU.mult).then_inc(s_w, 1)
            e.wait_ge(s_w, 1)
            e.wait_ge(s_pad, 3)

            def body(U):
                u = U.u

                def lo(*label):
                    ps, hi, dst = target(label, U.bank(*label))
                    e.wait_ge(s_hi, U.hi(*label))
                    if label[0] == "QT":
                        e.scalar_tensor_tensor(dst, ps, qkw[:, 2:3], f(hi), ALU.mult, ALU.subtract)\
                            .then_inc(s_free, 1)
                    else:
                        e.tensor_tensor(dst, ps, f(hi), ALU.subtract).then_inc(s_free, 1)

                def chunk_max(i, k):
                    at, to, c = ((0, 1024, 1), (1024, 1536, 2), (1536, NK, 3))[k]
                    e.wait_ge(s_sc, 4 * (NQ * u + i) + c + 1)
                    e.reduce_max(pm[:, i % 2, k:k + 1], S_ps[:, at:to], AX.X).then_inc(s_max, 1)

                def negate(i):
                    e.wait_ge(s_max, 3 * (NQ * u + i + 1))
                    e.tensor_reduce(nm[:, i % 2:i % 2 + 1], pm[:, i % 2, :], AX.X, ALU.max, negate=True)\
                        .then_inc(s_nm, 1)

                def norm_rows(i):
                    e.wait_ge(s_ri, NQ * u + i + 1)
                    p = prob[:, i % 2, 0:SPLIT]
                    e.tensor_scalar(p, p, rinv[:, i % 2, 1:2], None, ALU.mult).then_inc(s_pn, 1)

                def reciprocal(i):
                    e.wait_ge(s_exp, 2 * (NQ * u + i + 1))
                    e.tensor_tensor(rinv[:, i % 2, 0:1], rsum[:, i % 2, 0:1], rsum[:, i % 2, 1:2], ALU.add)\
                        .then_inc(s_rs, 1)
                    e.wait_ge(s_rs, NQ * u + i + 1)
                    e.reciprocal(rinv[:, i % 2, 1:2], rinv[:, i % 2, 0:1]).then_inc(s_ri, 1)

                def out_lo(g):
                    e.wait_ge(s_oh, GR * u + g + 1)
                    e.tensor_tensor(OT_lo[:, g, :], OT_ps[:, 0:TPB * P], f(OT_hi[:, g, :]), ALU.subtract)\
                        .then_inc(s_ol, 1)

                def norm(job):
                    no = JOBS.index(job)
                    n = job_no(U, job)
                    src = job_source(U, job)
                    k = src.shape[1]
                    rows = nat[:, no % 2, 0:k, :]
                    e.wait_ge(s_sq, n)
                    e.reduce_sum(nrm[:, 0, 0:k], rows, AX.X).then_inc(s_ss, 1)
                    e.wait_ge(s_ss, n)
                    e.tensor_scalar(nrm[:, 1, 0:k], nrm[:, 0, 0:k], 1.0 / HD, EPS, ALU.mult, ALU.add)\
                        .then_inc(s_ms, 1)
                    if job[0] == "KV" and job[1] > 0:
                        v_lo(job[1])
                    e.wait_ge(s_y0, n)
                    newton_rsqrt(e, nc, nrm[:, 1, 0:k], nrm[:, 3, 0:k], nrm[:, 4, 0:k], nrm[:, 5, 0:k],
                                 (s_nw, 3 * n - 3)).then_inc(s_nw, 1)
                    e.wait_ge(s_nw, 3 * n)
                    e.tensor_tensor(rows, src, nrm[:, 5, 0:k].unsqueeze(2).to_broadcast([P, k, HD]),
                                    ALU.mult).then_inc(s_nat, 1)
                    if job[0] == "Q":
                        e.wait_ge(s_nat, n)
                        e.sem_inc(s_free, 1)

                def v_lo(g):
                    e.wait_ge(s_vh, 4 * (u + 1) + g + 1)
                    at = slice(4 * g, 4 * g + len(SETS[g]))
                    e.tensor_tensor(V_lo[:, at, :], v_source(g), f(V_hi[:, at, :]), ALU.subtract)\
                        .then_inc(s_vl, 1)

                def add_output(t):
                    e.wait_ge(s_full, U.ring("O", t))
                    if t == 0:
                        e.wait_ge(s_yd, 32 * U.b + 16)
                    e.tensor_tensor(y[:, t, :], y[:, t, :], ring_ps[U.bank("O", t)][:], ALU.add)\
                        .then_inc(s_free, 1)

                if U.kind == START:
                    for n in range(NJ):
                        lo("X", n)
                    norm(("KV", 0))
                    v_lo(0)
                    lo("KT", 0)
                    norm(("KV", 1))
                    lo("KT", 1)
                else:
                    for i in range(1, NQ):
                        chunk_max(i, 0)
                        if i % 2 == 0 and U.kind != TURN:
                            lo("T", i - 2, 3)
                            if i >= 4:
                                out_lo((i - 4) // 2)
                        if i % 2 == 0:
                            lo("T", i - 1, 0)
                        chunk_max(i, 1)
                        chunk_max(i, 2)
                        negate(i)
                        if i % 2:
                            lo("T", i - 1, 0)
                        lo("T", i - 1, 1)
                        if i % 2 == 0:
                            lo("T", i - 1, 2)
                        reciprocal(i)
                        norm_rows(i)
                        if i % 2:
                            lo("T", i - 1, 2)
                        if i % 2 == 0 or i == NQ - 1 or U.kind == TURN:
                            lo("T", i - 1, 3)
                        if i % 2 and i >= 3 and (i == NQ - 1 or U.kind == TURN):
                            out_lo((i - 3) // 2)
                        if U.kind == TURN:
                            for n in X_IN_STEP[i]:
                                lo("X", n)
                    i = NQ - 1
                    lo("T", i, 0)
                    lo("T", i, 1)
                    if U.has_next():
                        norm(("KV", 0))
                    lo("T", i, 2)
                    lo("T", i, 3)
                    out_lo(GR - 1)
                    if U.has_next():
                        v_lo(0)
                        norm(("KV", 1))
                        lo("KT", 0)
                if U.has_next():
                    norm(("KV", 2))
                    if U.kind != START:
                        lo("KT", 1)
                    norm(("Q", 0))
                    lo("KT", 2)
                    lo("QT", 0)
                    norm(("KV", 3))
                    chunk_max(NQ, 0)
                    norm(("Q", 1))
                    lo("KT", 3)
                    chunk_max(NQ, 1)
                    chunk_max(NQ, 2)
                    negate(NQ)
                    if U.kind != START:
                        add_output(0)
                    lo("QT", 1)
                    if U.kind != START:
                        add_output(1)
                    reciprocal(NQ)
                    norm_rows(NQ)
                else:
                    add_output(0)
                    add_output(1)
            units(e, body)


def feed_forward(nc, y_in, Wr, rb, eb, out):
    B, S, E = y_in.shape
    NE = Wr.shape[0]
    C = E // P
    TPB = S // P
    TOP = 8

    with ExitStack() as ctx:
        def sb(name, shape, dt=F32):
            return ctx.enter_context(nc.sbuf_tensor(name, shape, dt))

        def sem(name):
            return ctx.enter_context(nc.semaphore(name))

        N = B * TPB

        def first_norm(n):
            return max(2 * n - 1, 0)

        def last_norm(n):
            return min(2 * n + 2, 2 * N - 1)

        y = sb("f_y", [P, N, E])
        z = sb("f_z", [P, N, E])
        xT = sb("f_xT", [P, 2, C, P])
        wr = sb("f_wr", [NE, E])
        wrT = sb("f_wrT", [P, C, NE])
        ebs = sb("f_eb", [NE, E])
        rbs = sb("f_rb", [1, NE])
        ones = sb("f_ones", [1, P])
        ident = sb("f_ident", [P, P])
        bn = sb("f_bn", [P, N, 6])
        mv = sb("f_mv", [P, N, 2])
        rs = sb("f_rs", [P, N, 5])
        soft = sb("f_soft", [P, N, 4])
        ex = sb("f_exp", [P, N, NE])
        rest = sb("f_rest", [P, N, NE])
        top = sb("f_top", [P, N, TOP])
        wT = sb("f_wT", [NE, 2, P])
        tr = [ctx.enter_context(nc.psum_tensor(f"f_tr{i}", [P, 512], F32)) for i in range(2)]
        lg = [ctx.enter_context(nc.psum_tensor(f"f_lg{i}", [P, 512], F32)) for i in range(2)]
        tw = [ctx.enter_context(nc.psum_tensor(f"f_tw{i}", [P, 512], F32)) for i in range(2)]
        mx = [ctx.enter_context(nc.psum_tensor(f"f_mx{i}", [P, 512], F32)) for i in range(2)]

        s_w = sem("f_weights_loaded")
        s_c = sem("f_constants")
        s_y = [sem(f"f_y_loaded{n}") for n in range(N)]
        s_wt = sem("f_router_transposed")
        s_wc = sem("f_router_copied")
        s_bn = sem("f_bn_steps")
        s_va = sem("f_variance")
        s_ln = sem("f_log_variance")
        s_y0 = sem("f_rsqrt_estimate")
        s_nw = sem("f_newton_steps")
        s_x2 = sem("f_x2")
        s_tr = sem("f_x2_transposed")
        s_xT = sem("f_x2T_copied")
        s_lg = sem("f_logits")
        s_nm = sem("f_negated_max")
        s_ex = sem("f_exponentials")
        s_sm = sem("f_softmax_steps")
        s_tk = sem("f_top_weights")
        s_tw = sem("f_weights_transposed")
        s_tc = sem("f_weights_copied")
        s_mx = sem("f_mixed")
        s_z = sem("f_z")
        s_ou = sem("f_normed")
        s_st = sem("f_stored")

        block = ctx.enter_context(nc.Block())
        yv = y_in.rearrange("b (t p) e -> p (b t) e", p=P)
        ov = out.rearrange("b (t p) e -> p (b t) e", p=P)

        @block.sync
        def _(e):
            e.dma_start(y[:, 0, :], yv[:, 0, :]).then_inc(s_y[0], 16)
            e.dma_start(wr[:], Wr).then_inc(s_w, 16)
            e.dma_start(ebs[:], eb).then_inc(s_w, 16)
            e.dma_start(rbs[:], rb.rearrange("(o n) -> o n", o=1)).then_inc(s_w, 16)
            for n in range(1, N):
                e.dma_start(y[:, n, :], yv[:, n, :]).then_inc(s_y[n], 16)
            for n in range(N):
                e.wait_ge(s_ou, n + 1)
                e.dma_start(ov[:, n, :], z[:, n, :]).then_inc(s_st, 16)
            e.wait_ge(s_st, 16 * N)

        @block.gpsimd
        def _(e):
            e.memset(ones[:], 1.0).then_inc(s_c, 1)
            e.memset(ident[:], 0.0).then_inc(s_c, 1)
            e.wait_ge(s_c, 2)
            e.affine_select(out=ident[:], in_=ident[:], compare_op=ALU.not_equal, fill=1.0, base=0,
                            pattern=[[-1, P]], channel_multiplier=1).then_inc(s_c, 1)

        @block.tensor
        def _(e):
            e.wait_ge(s_c, 3)
            e.wait_ge(s_w, 48)
            for c in range(C):
                ins = e.transpose(tw[0][:, c * NE:(c + 1) * NE], wr[:, c * P:(c + 1) * P], ident[0:NE, 0:NE])
            ins.then_inc(s_wt, 1)
            e.wait_ge(s_wc, 1)

            def logits(n):
                e.wait_ge(s_x2, n + 1)
                for c in range(C):
                    ins = e.transpose(tr[n % 2][:, c * P:(c + 1) * P], y[:, n, c * P:(c + 1) * P], ident[:])
                ins.then_inc(s_tr, 1)
                e.wait_ge(s_xT, n + 1)
                for c in range(C):
                    e.matmul(lg[n % 2][:, 0:NE], xT[:, n % 2, c, :], wrT[:, c, :], start=(c == 0), stop=False)
                e.matmul(lg[n % 2][:, 0:NE], ones[:], rbs[:], start=False, stop=True).then_inc(s_lg, 1)

            def mix(n):
                e.wait_ge(s_tk, 2 * n + 2)
                e.transpose(tw[n % 2][0:NE, 0:P], rest[:, n, :], ident[:]).then_inc(s_tw, 1)
                e.wait_ge(s_tc, n + 1)
                e.matmul(mx[n % 2][:], wT[:, n % 2, :], ebs[:], start=True, stop=True).then_inc(s_mx, 1)
            for n in range(N + 1):
                if n >= 1:
                    mix(n - 1)
                if n < N:
                    if n >= 2:
                        e.wait_ge(s_z, n - 1)
                    logits(n)

        @block.scalar
        def _(e):
            e.preload_act_table_set("natural_log_exp_and_others")
            e.wait_ge(s_wt, 1)
            e.activation(wrT[:], tw[0][:, 0:C * NE].rearrange("p (c n) -> p c n", n=NE), ACT.Copy)\
                .then_inc(s_wc, 1)

            def rsqrt(k, n):
                e.wait_ge(s_va, k + 1)
                e.activation(rs[:, n, 1:2], rs[:, n, 0:1], ACT.Ln).then_inc(s_ln, 1)
                e.wait_ge(s_ln, k + 1)
                e.activation(rs[:, n, 2:3], rs[:, n, 1:2], ACT.Exp, scale=-0.5).then_inc(s_y0, 1)
            for n in range(N + 1):
                if n < N:
                    rsqrt(first_norm(n), n)
                if n >= 1:
                    m = n - 1
                    e.wait_ge(s_tw, m + 1)
                    e.activation(wT[:, m % 2, :], tw[m % 2][0:NE, 0:P], ACT.Copy).then_inc(s_tc, 1)
                if n < N:
                    e.wait_ge(s_tr, n + 1)
                    e.activation(xT[:, n % 2].rearrange("p c k -> p (c k)"), tr[n % 2][:], ACT.Copy)\
                        .then_inc(s_xT, 1)
                if n >= 1:
                    rsqrt(last_norm(n - 1), n - 1)
                if n < N:
                    e.wait_ge(s_nm, n + 1)
                    e.activation(ex[:, n, :], lg[n % 2][:, 0:NE], ACT.Exp, bias=soft[:, n, 0:1],
                                 accum_out=soft[:, n, 1:2]).then_inc(s_ex, 1)

        @block.vector
        def _(e):
            bns = sms = 0

            def statistics(src, n):
                nonlocal bns
                e.bn_stats(bn[:, n, :], src).then_inc(s_bn, 1)
                e.wait_ge(s_bn, bns + 1)
                e.bn_aggr(mv[:, n, :], bn[:, n, :]).then_inc(s_bn, 1)
                e.wait_ge(s_bn, bns + 2)
                bns += 2
                e.tensor_scalar(rs[:, n, 0:1], mv[:, n, 1:2], 1e-5, None, ALU.add).then_inc(s_va, 1)

            def apply(k, src, dst, n, done):
                e.wait_ge(s_y0, k + 1)
                newton_rsqrt(e, nc, rs[:, n, 0:1], rs[:, n, 2:3], rs[:, n, 3:4], rs[:, n, 4:5],
                             (s_nw, 3 * k)).then_inc(s_nw, 1)
                e.wait_ge(s_nw, 3 * k + 3)
                e.tensor_scalar(dst, src, mv[:, n, 0:1], rs[:, n, 4:5], ALU.subtract, ALU.mult)\
                    .then_inc(done, 1)

            def weights(n):
                nonlocal sms
                e.wait_ge(s_lg, n + 1)
                e.tensor_reduce(soft[:, n, 0:1], lg[n % 2][:, 0:NE], AX.X, ALU.max, negate=True).then_inc(s_nm, 1)
                e.wait_ge(s_ex, n + 1)
                e.reciprocal(soft[:, n, 2:3], soft[:, n, 1:2]).then_inc(s_sm, 1)
                e.wait_ge(s_sm, sms + 1)
                e.tensor_scalar(ex[:, n, :], ex[:, n, :], soft[:, n, 2:3], None, ALU.mult).then_inc(s_sm, 1)
                e.wait_ge(s_sm, sms + 2)
                e.max(top[:, n, :], ex[:, n, :]).then_inc(s_sm, 1)
                e.wait_ge(s_sm, sms + 3)
                e.match_replace(rest[:, n, :], top[:, n, :], ex[:, n, :], 0.0).then_inc(s_sm, 1)
                e.reduce_sum(soft[:, n, 3:4], top[:, n, :], AX.X).then_inc(s_sm, 1)
                e.wait_ge(s_sm, sms + 5)
                sms += 5
                e.tensor_scalar(soft[:, n, 3:4], soft[:, n, 3:4], 1.0, None, ALU.add).then_inc(s_tk, 1)
                e.tensor_tensor(rest[:, n, :], ex[:, n, :], rest[:, n, :], ALU.subtract).then_inc(s_tk, 1)

            def combine(n):
                e.wait_ge(s_mx, n + 1)
                e.scalar_tensor_tensor(z[:, n, :], y[:, n, :], soft[:, n, 3:4], mx[n % 2][:], ALU.mult, ALU.add)\
                    .then_inc(s_z, 1)
                e.wait_ge(s_z, n + 1)
                statistics(z[:, n, :], n)

            for n in range(N + 1):
                if n < N:
                    e.wait_ge(s_y[n], 16)
                    statistics(y[:, n, :], n)
                    apply(first_norm(n), y[:, n, :], y[:, n, :], n, s_x2)
                if n >= 1:
                    combine(n - 1)
                    apply(last_norm(n - 1), z[:, n - 1, :], z[:, n - 1, :], n - 1, s_ou)
                if n < N:
                    weights(n)


def decoder_layer(nc, x, ctx_4096, sWq, sbq, sWk, sbk, sWv, sbv, xWq, xWk, xWv, xWo, xqw, xkw,
                  Wr, rb, eb, out):
    x1 = nc.dram_tensor("x1_scratch", x.shape, F32, kind="Internal").ap()
    x2 = nc.dram_tensor("x2_scratch", x.shape, F32, kind="Internal").ap()
    self_attention(nc, x, sWq, sbq, sWk, sbk, sWv, sbv, x1)
    cross_attention(nc, ctx_4096, xWq, xWk, xWv, xWo, xqw, xkw, x1, x2)
    feed_forward(nc, x2, Wr, rb, eb, out)


_INS = ["x", "ctx_4096", "L0_attn_Wq", "L0_attn_bq", "L0_attn_Wk", "L0_attn_bk", "L0_attn_Wv", "L0_attn_bv",
        "L0_xattn_Wq", "L0_xattn_Wk", "L0_xattn_Wv", "L0_xattn_Wo", "L0_xattn_q_norm_w",
        "L0_xattn_k_norm_w", "L0_ffn_router_weight", "L0_ffn_router_bias", "L0_ffn_expert_bias"]


def kernel(**inputs):
    import numpy as _np
    import concourse.bacc as _bacc
    from concourse import mybir as _mybir
    from concourse.bass_utils import run_bass_kernel_spmd as _run

    nc = _bacc.Bacc("TRN2", target_bir_lowering=False, num_devices=1)
    arrays, args = {}, []
    for name in _INS:
        a = _np.ascontiguousarray(inputs[name])
        arrays[f"in_{name}"] = a
        args.append(nc.dram_tensor(f"in_{name}", a.shape, _mybir.dt.from_np(a.dtype), kind="ExternalInput").ap())
    out = nc.dram_tensor("out_0", inputs["x"].shape, _mybir.dt.float32, kind="ExternalOutput").ap()
    decoder_layer(nc, *args, out)
    r = _run(nc, [arrays], core_ids=[0])
    return r.results[0]["out_0"]
```

```python
from contextlib import ExitStack

import concourse.bass as bass
from concourse import mybir

F32 = mybir.dt.float32
F32R = mybir.dt.float32r
ALU = mybir.AluOpType
ACT = mybir.ActivationFunctionType
AX = mybir.AxisListType
P = 128


def f(ap):
    return ap.bitcast(F32)


def newton_rsqrt(e, nc, x, y0, a, out, step):
    sem, n = step
    e.scalar_tensor_tensor(a, x, -0.5, y0, ALU.mult, ALU.mult).then_inc(sem, 1)
    e.wait_ge(sem, n + 1)
    e.tensor_tensor(a, a, y0, ALU.mult).then_inc(sem, 1)
    e.wait_ge(sem, n + 2)
    return e.scalar_tensor_tensor(out, a, 1.5, y0, ALU.add, ALU.mult)


def self_attention(nc, x, Wq, bq, Wk, bk, Wv, bv, x1):
    B, S, E = x.shape
    D, H = Wq.shape[1:]
    G = Wk.shape[2]
    R = H // G
    C = E // P
    DG = D * G
    NT = 4
    TURNS = B * S // P // NT
    PAIRS = [list(range(t, t + 2)) for t in range(0, NT, 2)]
    DD = 4
    assert TURNS * NT * P == B * S
    xf = x.rearrange("b s e -> (b s) e")
    x1f = x1.rearrange("b s e -> (b s) e")

    with ExitStack() as ctx:
        def sb(name, shape, dt=F32):
            return ctx.enter_context(nc.sbuf_tensor(name, shape, dt))

        def sem(name):
            return ctx.enter_context(nc.semaphore(name))

        w_raw = sb("a_w_raw", [P, C, E])
        w = sb("a_w", [P, C, 3 * DG])
        b_raw = sb("a_b_raw", [1, E])
        bias = sb("a_bias", [1, 3 * DG])
        ones = sb("a_ones", [1, P])
        ident = sb("a_ident", [P, P])
        xt = sb("a_x", [P, NT, E])
        xT = sb("a_xT", [P, NT, C, P])
        qkv = sb("a_qkv", [P, NT, 3 * DG])
        prod = sb("a_prod", [P, NT, D * D * G])
        sc = sb("a_scores", [P, NT, D, D])
        stat = sb("a_stat", [P, NT, 3, D])
        o = sb("a_o", [P, NT, DG])
        bn = sb("a_bn", [P, NT, 6])
        mv = sb("a_mv", [P, NT, 2])
        rs = sb("a_rs", [P, NT, 5])
        tr = [ctx.enter_context(nc.psum_tensor(f"a_tr{i}", [P, C, P], F32)) for i in range(NT)]
        pq = [ctx.enter_context(nc.psum_tensor(f"a_pq{i}", [P, 512], F32)) for i in range(NT)]

        s_w = sem("a_w_loaded")
        s_wr = sem("a_w_reduced")
        s_cst = sem("a_constants")
        s_x = [sem(f"a_x_loaded{i}") for i in range(NT)]
        s_tr = sem("a_transposed")
        s_xT = sem("a_xT_copied")
        s_pq = sem("a_projected")
        s_qkv = sem("a_qkv_copied")
        s_p1 = sem("a_qk_products")
        s_d1 = sem("a_qk_products_of_DVE")
        s_sc = sem("a_scores_summed")
        s_mx = sem("a_row_max")
        s_sh = sem("a_scores_shifted")
        s_ex = sem("a_exponentials")
        s_su = sem("a_row_sums")
        s_ri = sem("a_row_reciprocals")
        s_pr = sem("a_probabilities")
        s_p2 = sem("a_pv_products")
        s_d2 = sem("a_pv_products_of_DVE")
        s_o = sem("a_outputs_summed")
        s_h = sem("a_residual_added")
        s_bn = sem("a_bn_steps")
        s_go = sem("a_statistics_seen")
        s_va = sem("a_variance")
        s_ln = sem("a_log_variance")
        s_y0 = sem("a_rsqrt_estimate")
        s_nw = sem("a_newton_steps")
        s_x1 = sem("a_normalised")
        s_st = [sem(f"a_x1_stored{i}") for i in range(NT)]

        block = ctx.enter_context(nc.Block())

        @block.sync
        def _(e):
            with e.Fori(0, TURNS) as i:
                for t in range(NT):
                    e.wait_ge(s_st[t], 16 * i + 16)
                    e.dma_start(xt[:, t, :], xf[bass.ds((NT * i + t) * P, P), :]).then_inc(s_x[t], 16)
                for t in range(NT):
                    e.wait_ge(s_x1, NT * i + t + 1)
                    e.dma_start(x1f[bass.ds((NT * i + t) * P, P), :], xt[:, t, :]).then_inc(s_st[t], 16)
            for t in range(NT):
                e.wait_ge(s_st[t], 16 * TURNS + 16)

        def qk_products(e, t, ds):
            n = ds.stop - ds.start
            q = qkv[:, t, 0:DG].rearrange("p (d g) -> p d g", g=G)[:, ds]
            k = qkv[:, t, DG:2 * DG].rearrange("p (e g) -> p e g", g=G)
            return e.tensor_tensor(prod[:, t, :].rearrange("p (d e g) -> p d e g", d=D, e=D)[:, ds],
                                   q.unsqueeze(2).to_broadcast([P, n, D, G]),
                                   k.unsqueeze(1).to_broadcast([P, n, D, G]), ALU.mult)

        def pv_products(e, t, ds):
            n = ds.stop - ds.start
            v = qkv[:, t, 2 * DG:].rearrange("p (e g) -> p g e", g=G)
            return e.tensor_tensor(prod[:, t, :].rearrange("p (d g e) -> p d g e", d=D, g=G)[:, ds],
                                   sc[:, t, ds].unsqueeze(2).to_broadcast([P, n, G, D]),
                                   v.unsqueeze(1).to_broadcast([P, n, G, D]), ALU.mult)

        @block.gpsimd
        def _(e):
            for t in range(NT):
                e.sem_inc(s_st[t], 16)
            e.memset(ones[:], 1.0).then_inc(s_cst, 1)
            e.memset(ident[:], 0.0).then_inc(s_cst, 1)
            e.wait_ge(s_cst, 2)
            e.affine_select(out=ident[:], in_=ident[:], compare_op=ALU.not_equal, fill=1.0, base=0,
                            pattern=[[-1, P]], channel_multiplier=1).then_inc(s_cst, 1)
            with e.Fori(0, TURNS) as i:
                for t in range(NT):
                    e.wait_ge(s_qkv, NT * i + t + 1)
                    qk_products(e, t, slice(DD, D)).then_inc(s_p1, 1)
                for t in range(NT):
                    e.wait_ge(s_pr, NT * i + t + 1)
                    pv_products(e, t, slice(DD, D)).then_inc(s_p2, 1)

        @block.tensor
        def _(e):
            e.wait_ge(s_cst, 3)
            e.wait_ge(s_wr, 2)
            e.wait_ge(s_w, 96)
            with e.Fori(0, TURNS) as i:
                for t in range(NT):
                    e.wait_ge(s_x[t], 16 * i + 16)
                    for c in range(C):
                        ins = e.transpose(tr[t][:, c, :], xt[:, t, c * P:(c + 1) * P], ident[:])
                    ins.then_inc(s_tr, 1)
                for t in range(NT):
                    e.wait_ge(s_xT, NT * i + t + 1)
                    for c in range(C):
                        e.matmul(pq[t][:, 0:3 * DG], xT[:, t, c, :], w[:, c, :], start=(c == 0), stop=False)
                    e.matmul(pq[t][:, 0:3 * DG], ones[:], bias[:], start=False, stop=True).then_inc(s_pq, 1)

        @block.scalar
        def _(e):
            e.dma_start(w_raw[:], Wq.rearrange("(c p) d h -> p c (d h)", p=P)).then_inc(s_w, 16)
            e.dma_start(w[:, :, DG:2 * DG], Wk.rearrange("(c p) d g -> p c (d g)", p=P)).then_inc(s_w, 16)
            e.dma_start(w[:, :, 2 * DG:], Wv.rearrange("(c p) d g -> p c (d g)", p=P)).then_inc(s_w, 16)
            e.dma_start(b_raw[:], bq.rearrange("(o d) h -> o (d h)", o=1)).then_inc(s_w, 16)
            e.dma_start(bias[:, DG:2 * DG], bk.rearrange("(o d) g -> o (d g)", o=1)).then_inc(s_w, 16)
            e.dma_start(bias[:, 2 * DG:], bv.rearrange("(o d) g -> o (d g)", o=1)).then_inc(s_w, 16)
            e.preload_act_table_set("natural_log_exp_and_others")

            def project(i, t):
                n = NT * i + t + 1
                e.wait_ge(s_pq, n)
                e.activation(qkv[:, t, :], pq[t][:, 0:3 * DG], ACT.Copy).then_inc(s_qkv, 1)

            with e.Fori(0, TURNS) as i:
                for t in range(NT):
                    e.wait_ge(s_tr, NT * i + t + 1)
                    e.activation(xT[:, t], tr[t][:], ACT.Copy).then_inc(s_xT, 1)
                for t in range(NT):
                    project(i, t)
                for t in range(NT):
                    e.wait_ge(s_sh, NT * i + t + 1)
                    e.activation(sc[:, t], sc[:, t], ACT.Exp, scale=float(D) ** -0.5).then_inc(s_ex, 1)
                for t in range(NT):
                    n = NT * i + t + 1
                    e.wait_ge(s_va, n)
                    e.activation(rs[:, t, 1:2], rs[:, t, 0:1], ACT.Ln).then_inc(s_ln, 1)
                    e.wait_ge(s_ln, n)
                    e.activation(rs[:, t, 2:3], rs[:, t, 1:2], ACT.Exp, scale=-0.5).then_inc(s_y0, 1)

        @block.vector
        def _(e):
            e.wait_ge(s_w, 96)
            e.reduce_sum(w[:, :, 0:DG], w_raw[:].rearrange("p c (n r) -> p c n r", r=R), AX.X).then_inc(s_wr, 1)
            e.reduce_sum(bias[:, 0:DG], b_raw[:].rearrange("p (n r) -> p n r", r=R), AX.X).then_inc(s_wr, 1)
            with e.Fori(0, TURNS) as i:
                def products(t):
                    e.wait_ge(s_qkv, NT * i + t + 1)
                    qk_products(e, t, slice(0, DD)).then_inc(s_d1, 1)

                def scores(t):
                    n = NT * i + t + 1
                    e.wait_ge(s_p1, n)
                    e.wait_ge(s_d1, n)
                    e.reduce_sum(sc[:, t], prod[:, t, :].rearrange("p (d e g) -> p d e g", d=D, e=D), AX.X)\
                        .then_inc(s_sc, 1)
                    e.wait_ge(s_sc, n)
                    e.reduce_max(stat[:, t, 0, :], sc[:, t], AX.X).then_inc(s_mx, 1)
                    e.wait_ge(s_mx, n)
                    e.tensor_tensor(sc[:, t], sc[:, t], stat[:, t, 0, :].unsqueeze(2).to_broadcast([P, D, D]),
                                    ALU.subtract).then_inc(s_sh, 1)

                def normalise(t):
                    n = NT * i + t + 1
                    e.wait_ge(s_ex, n)
                    e.reduce_sum(stat[:, t, 1, :], sc[:, t], AX.X).then_inc(s_su, 1)
                    e.wait_ge(s_su, n)
                    e.reciprocal(stat[:, t, 2, :], stat[:, t, 1, :]).then_inc(s_ri, 1)
                    e.wait_ge(s_ri, n)
                    e.tensor_tensor(sc[:, t], sc[:, t], stat[:, t, 2, :].unsqueeze(2).to_broadcast([P, D, D]),
                                    ALU.mult).then_inc(s_pr, 1)
                    e.wait_ge(s_pr, n)
                    pv_products(e, t, slice(0, DD)).then_inc(s_d2, 1)

                def residual(t):
                    n = NT * i + t + 1
                    e.wait_ge(s_p2, n)
                    e.wait_ge(s_d2, n)
                    e.reduce_sum(o[:, t, :], prod[:, t, :].rearrange("p (n e) -> p n e", e=D), AX.X)\
                        .then_inc(s_o, 1)
                    e.wait_ge(s_o, n)
                    h = xt[:, t, :].rearrange("p (n r) -> p n r", r=R)
                    e.tensor_tensor(h, h, o[:, t, :].unsqueeze(2).to_broadcast([P, DG, R]), ALU.add)\
                        .then_inc(s_h, 1)
                    e.wait_ge(s_h, n)
                    e.bn_stats(bn[:, t, :], xt[:, t, :]).then_inc(s_bn, 1)
                    e.wait_ge(s_bn, 2 * n - 1)
                    e.sem_inc(s_go, 1)
                    e.bn_aggr(mv[:, t, :], bn[:, t, :]).then_inc(s_bn, 1)
                    e.wait_ge(s_bn, 2 * n)
                    e.tensor_scalar(rs[:, t, 0:1], mv[:, t, 1:2], 1e-5, None, ALU.add).then_inc(s_va, 1)

                def layernorm(t):
                    n = NT * i + t + 1
                    e.wait_ge(s_y0, n)
                    newton_rsqrt(e, nc, rs[:, t, 0:1], rs[:, t, 2:3], rs[:, t, 3:4], rs[:, t, 4:5],
                                 (s_nw, 3 * n - 3)).then_inc(s_nw, 1)
                    e.wait_ge(s_nw, 3 * n)
                    e.tensor_scalar(xt[:, t, :], xt[:, t, :], mv[:, t, 0:1], rs[:, t, 4:5],
                                    ALU.subtract, ALU.mult).then_inc(s_x1, 1)

                for pair in PAIRS:
                    for step in (products, scores, normalise):
                        for t in pair:
                            step(t)
                for step in (residual, layernorm):
                    for t in range(NT):
                        step(t)


START, MID, TURN, LAST = "start", "mid", "turn", "last"


def cross_attention(nc, ctx_in, Wq, Wk, Wv, Wo, qw, kw, x1, y_out):
    B, L, E = ctx_in.shape
    S = x1.shape[1]
    HD = P
    KVH = Wk.shape[1] // HD
    GR = Wq.shape[1] // HD // KVH
    C = E // P
    TPB = S // P
    NK = L + S
    NJ = -(-NK // P)
    TAIL = NK - (NJ - 1) * P
    NKP = NJ * P
    NQ = GR * TPB
    CH = [(c * 512, min(512, NK - c * 512)) for c in range(-(-NK // 512))]
    CH = [(o, n + n % 2) for o, n in CH]
    SETS = [list(range(4 * s, min(4 * s + 4, NJ))) for s in range(-(-NJ // 4))]
    assert TPB == 2 and GR == 4 and C == 4 and len(CH) == 4 and len(SETS) == 4 and NQ == 8
    SPLIT = 512
    FIRST = 6
    H1 = 8
    EPS = 1e-6

    X_IN_STEP = {i: [n for n in range(NJ) if n * (NQ - 1) // NJ + 1 == i] for i in range(1, NQ)}

    def ring_order(kind):
        order = []
        if kind == START:
            order += [("X", n) for n in range(NJ)]
        else:
            for i in range(1, NQ):
                order += [("T", i - 1, s) for s in range(4)]
                if kind == TURN:
                    order += [("X", n) for n in X_IN_STEP[i]]
            order += [("T", NQ - 1, s) for s in range(4)]
        if kind == LAST:
            return order + [("O", 0), ("O", 1)]
        order += [("KT", 0), ("KT", 1), ("Q", 0), ("KT", 2), ("QT", 0), ("Q", 1), ("KT", 3), ("O", 0),
                  ("QT", 1), ("O", 1)]
        return [x for x in order if kind != START or x[0] != "O"]

    RING = {k: ring_order(k) for k in (START, MID, TURN, LAST)}
    FREE = {k: [x for x in v if x[0] != "Q"] for k, v in RING.items()}
    HI = {k: [x for x in v if x[0] in ("X", "T", "KT", "QT")] for k, v in RING.items()}
    assert len(RING[MID]) % 3 == 0 and len(RING[TURN]) % 3 == 0

    class Unit:

        def __init__(self, kind, b, h):
            self.kind, self.b, self.h = kind, b, h
            self.u = -1 if kind == START else b * KVH + h

            def before(table):
                if kind == START:
                    return 0
                per_batch = (KVH - 1) * len(table[MID]) + len(table[TURN])
                return len(table[START]) + b * per_batch + h * len(table[MID])
            self.ring0, self.free0, self.hi0 = before(RING), before(FREE), before(HI)

        def ring(self, *label):
            return self.ring0 + RING[self.kind].index(label) + 1

        def free(self, *label):
            return self.free0 + FREE[self.kind].index(label) + 1

        def left(self, *label):
            at = RING[self.kind].index(label) - 3
            if at < 0:
                return self.free0 + at + 1
            return self.free0 + sum(x[0] != "Q" for x in RING[self.kind][:at + 1])

        def hi(self, *label):
            return self.hi0 + HI[self.kind].index(label) + 1

        def bank(self, *label):
            first = 0 if self.kind == START else len(RING[START])
            return (first + RING[self.kind].index(label)) % 3

        def has_next(self):
            return self.kind != LAST

    def units(e, body):
        body(Unit(START, 0, 0))
        with e.Fori(0, B - 1) as b:
            with e.Fori(0, KVH - 1) as h:
                body(Unit(MID, b, h))
            body(Unit(TURN, b, KVH - 1))
        with e.Fori(0, KVH - 1) as h:
            body(Unit(MID, B - 1, h))
        body(Unit(LAST, B - 1, KVH - 1))

    with ExitStack() as ctx:
        def sb(name, shape, dt=F32):
            return ctx.enter_context(nc.sbuf_tensor(name, shape, dt))

        def sem(name):
            return ctx.enter_context(nc.semaphore(name))

        def pair(name, shape):
            return sb(name + "_hi", shape, F32R), sb(name + "_lo", shape, F32R)

        kvT_hi, kvT_lo = pair("kvT", [P, C, NKP])
        KT_hi, KT_lo = pair("KT", [P, NKP])
        V_hi, V_lo = pair("V", [P, NJ, HD])
        PT_hi, PT_lo = pair("PT", [P, NJ, TPB * P])
        QT_hi, QT_lo = pair("QT", [P, GR, TPB * P])
        OT_hi, OT_lo = pair("OT", [P, GR, TPB * P])
        Wkv_hi, Wkv_lo = pair("Wkv", [P, C, 2 * HD])
        Wq_hi, Wq_lo = pair("Wq", [P, C, GR * HD])
        Wo_hi, Wo_lo = pair("Wo", [P, GR, E])
        stage = sb("w_stage", [P, 1024])
        prob = sb("prob", [P, 2, NKP])
        nat = sb("nat", [P, 2, 4, HD])
        y = sb("y", [P, TPB, E])
        ident = sb("ident", [P, P])
        one = sb("one", [P, 1])
        qkw = sb("qkw", [P, 3])
        pm = sb("pm", [P, 2, 3])
        nm = sb("nm", [P, 2])
        rsum = sb("rsum", [P, 2, 2])
        rinv = sb("rinv", [P, 2, 2])
        nrm = sb("nrm", [P, 6, 4])

        S_ps = ctx.enter_context(nc.psum_tensor("S_ps", [P, 4 * 512], F32))
        ring_ps = [ctx.enter_context(nc.psum_tensor(f"ring{i}", [P, 512], F32)) for i in range(3)]
        OT_ps = ctx.enter_context(nc.psum_tensor("OT_ps", [P, 512], F32))
        KV_ps = S_ps[:].rearrange("p (a n) -> p a n", n=2 * HD)

        s_id = sem("identity")
        s_pad = sem("pads_zeroed")
        s_qkw = sem("norm_weights_loaded")
        s_w = sem("norm_weight_ready")
        s_wd = sem("weights_loaded")
        s_ws = sem("weights_split")
        s_xd = [sem(f"key_rows_loaded{i}") for i in range(2)]
        s_xf = [sem(f"first_key_rows_loaded{i}") for i in range(FIRST)]
        s_yd = sem("y_moved")
        s_full = sem("ring_full")
        s_free = sem("ring_free")
        s_hi = sem("ring_hi_copied")
        s_sc = sem("scores_full")
        s_max = sem("chunk_max")
        s_nm = sem("negated_max")
        s_exp = sem("exponentials")
        s_rs = sem("row_sum")
        s_ri = sem("row_reciprocal")
        s_pn = sem("left_probabilities_normed")
        s_pa = sem("right_probabilities_normed")
        s_of = sem("OT_full")
        s_oh = sem("OT_hi_copied")
        s_ol = sem("OT_lo_copied")
        s_kv = sem("KV_full")
        s_sq = sem("squares")
        s_ss = sem("sum_of_squares")
        s_ms = sem("mean_square")
        s_ln = sem("log_mean_square")
        s_y0 = sem("rsqrt_estimate")
        s_nw = sem("newton_steps")
        s_nat = sem("rows_normed")
        s_vh = sem("V_hi_copied")
        s_vl = sem("V_lo_copied")

        block = ctx.enter_context(nc.Block())

        def target(label, bank):
            ps = ring_ps[bank][:]
            if label[0] == "T":
                _, i, s = label
                n, q = len(SETS[s]), (i % TPB) * P
                return (ps[:, 0:n * P].rearrange("p (j q) -> p j q", q=P),
                        PT_hi[:, 4 * s:4 * s + n, q:q + P], PT_lo[:, 4 * s:4 * s + n, q:q + P])
            if label[0] == "KT":
                n = len(SETS[label[1]]) * P
                at = label[1] * 512
                return ps[:, 0:n], KT_hi[:, at:at + n], KT_lo[:, at:at + n]
            if label[0] == "QT":
                q = label[1] * P
                return (ps.rearrange("p (h q) -> p h q", q=P), QT_hi[:, :, q:q + P], QT_lo[:, :, q:q + P])
            n = label[1]
            rows = P if n < NJ - 1 else TAIL
            return (ps.rearrange("p (c k) -> p c k", k=P)[:, :, 0:rows],
                    kvT_hi[:, :, n * P:n * P + rows], kvT_lo[:, :, n * P:n * P + rows])

        def key_rows(kind, n):
            if kind == START:
                m = n % FIRST
                return prob[:, m // 3, m % 3 * E:(m % 3 + 1) * E]
            return nat[:, n % 2].rearrange("p c d -> p (c d)")

        JOBS = [("KV", 0), ("KV", 1), ("KV", 2), ("Q", 0), ("KV", 3), ("Q", 1)]
        OUT = {("KV", g): ("KT", g) for g in range(4)} | {("Q", t): ("QT", t) for t in range(TPB)}

        def job_no(U, job):
            return 6 * (U.u + 1) + JOBS.index(job) + 1

        def job_source(U, job):
            if job[0] == "Q":
                return ring_ps[U.bank(*job)][:].rearrange("p (h d) -> p h d", d=HD)
            g = job[1]
            a = 4 * (g % 2)
            return KV_ps[:, a:a + len(SETS[g]), 0:HD]

        def v_source(g):
            a = 4 * (g % 2)
            return KV_ps[:, a:a + len(SETS[g]), HD:2 * HD]

        def weights_split(U, n):
            return 2 * n if U.kind == START else 2 * (3 + 5 * U.u + n)

        @block.sync
        def _(e):
            e.dma_start(qkw[:, 0:1], qw.rearrange("(p o) -> p o", o=1)).then_inc(s_qkw, 16)
            e.dma_start(qkw[:, 1:2], kw.rearrange("(p o) -> p o", o=1)).then_inc(s_qkw, 16)
            e.dma_start(y[:], x1[0].rearrange("(t p) e -> p t e", p=P)).then_inc(s_yd, 16)
            wk = Wk.rearrange("(c p) n -> p c n", p=P)
            wv = Wv.rearrange("(c p) n -> p c n", p=P)
            wq = Wq.rearrange("(c p) n -> p c n", p=P)
            wo = Wo.rearrange("(g p) n -> p g n", p=P)

            def body(U):
                job = 0

                def free(n):
                    if not (U.kind == START and n == 0):
                        e.wait_ge(s_ws, weights_split(U, n))
                if U.has_next():
                    h = 0 if U.kind in (START, TURN) else U.h + 1
                    st = stage[:].rearrange("p (c n) -> p c n", c=C)
                    free(0)
                    e.dma_start(st[:, :, 0:HD], wk[:, :, bass.ts(h, HD)]).then_inc(s_wd, 16)
                    e.dma_start(st[:, :, HD:2 * HD], wv[:, :, bass.ts(h, HD)]).then_inc(s_wd, 16)
                    for a in range(2):
                        free(1 + a)
                        e.dma_start(stage[:].rearrange("p (c n) -> p c n", c=2),
                                    wq[:, 2 * a:2 * a + 2, bass.ts(h, GR * HD)]).then_inc(s_wd, 16)
                    job = 3
                if U.kind != START:
                    for a in range(2):
                        free(job + a)
                        e.dma_start(stage[:].rearrange("p (c n) -> p c n", c=2),
                                    wo[:, bass.ds(U.h * GR + 2 * a, 2), :]).then_inc(s_wd, 16)
                if U.kind in (TURN, LAST):
                    e.wait_ge(s_free, U.free("O", 1))
                    e.dma_start(y_out[bass.ds(U.b, 1)].rearrange("o (t p) e -> p (o t) e", p=P), y[:])\
                        .then_inc(s_yd, 16)
                    e.wait_ge(s_yd, 32 * U.b + 32)
                if U.kind == TURN:
                    e.dma_start(y[:], x1[bass.ds(U.b + 1, 1)].rearrange("o (t p) e -> p (o t) e", p=P))\
                        .then_inc(s_yd, 16)
            units(e, body)

        @block.gpsimd
        def _(e):
            e.sem_inc(s_ol, 1)
            e.memset(ident[:], 0.0).then_inc(s_id, 1)
            e.wait_ge(s_id, 1)
            e.affine_select(out=ident[:], in_=ident[:], compare_op=ALU.not_equal, fill=1.0, base=0,
                            pattern=[[-1, P]], channel_multiplier=1).then_inc(s_id, 1)
            e.memset(one[:], 1.0).then_inc(s_id, 1)
            e.memset(f(kvT_hi[:, :, NK:NKP]), 0.0).then_inc(s_pad, 1)
            e.memset(f(kvT_lo[:, :, NK:NKP]), 0.0).then_inc(s_pad, 1)
            e.memset(prob[:, :, NK:NKP], 0.0).then_inc(s_pad, 1)

            def body(U):
                dmas = 0 if U.kind == START else 16 * (4 + 6 * U.u)
                n = 0
                if U.kind == START:
                    e.wait_ge(s_id, 3)
                else:
                    e.wait_ge(s_full, U.ring0)

                def split(src, hi, lo, loads):
                    nonlocal dmas, n
                    dmas = dmas + 16 * loads
                    e.wait_ge(s_wd, dmas)
                    e.tensor_tensor(hi, src, one[:].unsqueeze(2).to_broadcast(list(src.shape)), ALU.mult).then_inc(s_ws, 1)
                    e.wait_ge(s_ws, weights_split(U, n) + 1)
                    e.tensor_tensor(lo, src, f(hi), ALU.subtract).then_inc(s_ws, 1)
                    n += 1
                if U.has_next():
                    split(stage[:].rearrange("p (c n) -> p c n", c=C), Wkv_hi[:], Wkv_lo[:], 2)
                    for a in range(2):
                        split(stage[:].rearrange("p (c n) -> p c n", c=2),
                              Wq_hi[:, 2 * a:2 * a + 2, :], Wq_lo[:, 2 * a:2 * a + 2, :], 1)
                if U.kind != START:
                    for a in range(2):
                        split(stage[:].rearrange("p (c n) -> p c n", c=2),
                              Wo_hi[:, 2 * a:2 * a + 2, :], Wo_lo[:, 2 * a:2 * a + 2, :], 1)
            units(e, body)

        @block.tensor
        def _(e):
            e.wait_ge(s_id, 2)
            e.wait_ge(s_pad, 3)

            def three(out, l_hi, l_lo, r_hi, r_lo, first, last):
                e.matmul(out, l_hi, r_hi, start=first, stop=False)
                e.matmul(out, l_hi, r_lo, start=False, stop=False)
                return e.matmul(out, l_lo, r_hi, start=False, stop=last)

            def body(U):
                u = U.u

                def take(*label):
                    if not (U.kind == START and RING[START].index(label) < 3):
                        e.wait_ge(s_free, U.left(*label))
                    return ring_ps[U.bank(*label)][:]

                def rows_in(n):
                    if U.kind == START:
                        e.wait_ge(s_xf[n % FIRST], 16 * (n // FIRST + 1))
                    else:
                        before = U.b * len(range(n % 2, NJ, 2))
                        e.wait_ge(s_xd[n % 2], 16 * (before + n // 2 + 1))
                    ps = take("X", n)
                    rows = P if n < NJ - 1 else TAIL
                    for c in range(C):
                        ins = e.transpose(ps[:, c * P:c * P + rows], key_rows(U.kind, n)[0:rows, c * P:(c + 1) * P],
                                          ident[0:rows, 0:rows])
                    ins.then_inc(s_full, 1)

                def scores(i, c):
                    at, n = CH[c]
                    g, q = i % NQ // TPB, (i % TPB) * P
                    if i == NQ:
                        if c == 0:
                            e.wait_ge(s_free, U.free("QT", 0))
                            e.wait_ge(s_nat, job_no(U, ("KV", 2)))
                            e.wait_ge(s_vl, 4 * (u + 1) + 3)
                        elif c == 2:
                            e.wait_ge(s_free, U.free("KT", 2))
                            e.wait_ge(s_nat, job_no(U, ("KV", 3)))
                            e.wait_ge(s_vl, 4 * (u + 1) + 4)
                        elif c == 3:
                            e.wait_ge(s_free, U.free("KT", 3))
                    elif c <= 1:
                        e.wait_ge(s_exp, 2 * (NQ * u + i - 1) + 1 + c)
                    three(S_ps[:, c * 512:c * 512 + n], QT_hi[:, g, q:q + P], QT_lo[:, g, q:q + P],
                          KT_hi[:, at:at + n], KT_lo[:, at:at + n], True, True).then_inc(s_sc, 1)

                def turn(i, s):
                    if s == 0:
                        e.wait_ge(s_pn, NQ * u + i + 1)
                    if s == SPLIT // 512:
                        e.wait_ge(s_pa, NQ * u + i + 1)
                    ps = take("T", i, s)
                    for k, j in enumerate(SETS[s]):
                        ins = e.transpose(ps[:, k * P:(k + 1) * P], prob[:, i % 2, j * P:(j + 1) * P], ident[:])
                    ins.then_inc(s_full, 1)

                def pv(g, js):
                    for j in js:
                        if j == 0:
                            e.wait_ge(s_ol, GR * u + g + 1)
                        if j % 4 == 0:
                            e.wait_ge(s_free, U.free("T", TPB * g + 1, j // 4))
                        ins = three(OT_ps[:, 0:TPB * P], V_hi[:, j, :], V_lo[:, j, :],
                                    PT_hi[:, j, :], PT_lo[:, j, :], j == 0, j == NJ - 1)
                    if js[-1] == NJ - 1:
                        ins.then_inc(s_of, 1)

                def kv(g, ks):
                    if ks[0] == SETS[g][0]:
                        if g == 0:
                            e.wait_ge(s_ws, weights_split(U, 1))
                        if U.kind in (START, TURN):
                            e.wait_ge(s_free, U.free("X", SETS[g][-1]))
                        if g < 2:
                            if U.kind != START:
                                e.wait_ge(s_exp, 2 * NQ * (u + 1))
                        else:
                            e.wait_ge(s_nat, job_no(U, ("KV", g - 2)))
                            e.wait_ge(s_vl, 4 * (u + 1) + g - 1)
                    for j in ks:
                        out = KV_ps[:, 4 * (g % 2) + j % 4, :]
                        for c in range(C):
                            ins = three(out, kvT_hi[:, c, j * P:(j + 1) * P], kvT_lo[:, c, j * P:(j + 1) * P],
                                        Wkv_hi[:, c, :], Wkv_lo[:, c, :], c == 0, c == C - 1)
                    if ks[-1] == SETS[g][-1]:
                        ins.then_inc(s_kv, 1)

                def queries(t):
                    if t == 0:
                        e.wait_ge(s_ws, weights_split(U, 3))
                    if t == 1:
                        e.wait_ge(s_nat, job_no(U, ("Q", 0)))
                    ps = take("Q", t)
                    for c in range(C):
                        ins = three(ps, kvT_hi[:, c, t * P:(t + 1) * P], kvT_lo[:, c, t * P:(t + 1) * P],
                                    Wq_hi[:, c, :], Wq_lo[:, c, :], c == 0, c == C - 1)
                    ins.then_inc(s_full, 1)

                def rows_out(job):
                    e.wait_ge(s_nat, job_no(U, job))
                    ps = take(*OUT[job])
                    n = GR if job[0] == "Q" else len(SETS[job[1]])
                    for k in range(n):
                        ins = e.transpose(ps[:, k * P:(k + 1) * P], nat[:, JOBS.index(job) % 2, k, :], ident[:])
                    ins.then_inc(s_full, 1)

                def output(t, gs):
                    if (t, gs[0]) == (0, 0):
                        e.wait_ge(s_ws, weights_split(U, 5 if U.has_next() else 2))
                        e.wait_ge(s_ol, GR * (u + 1) + 1)
                    ps = take("O", t) if gs[0] == 0 else ring_ps[U.bank("O", t)][:]
                    for g in gs:
                        ins = three(ps, OT_hi[:, g, t * P:(t + 1) * P], OT_lo[:, g, t * P:(t + 1) * P],
                                    Wo_hi[:, g, :], Wo_lo[:, g, :], g == 0, g == GR - 1)
                    if gs[-1] == GR - 1:
                        ins.then_inc(s_full, 1)

                first_half, rest = list(range(H1)), list(range(H1, NJ))
                if U.kind == START:
                    for n in range(H1):
                        rows_in(n)
                    kv(0, SETS[0])
                    for n in range(H1, NJ):
                        rows_in(n)
                    kv(1, SETS[1])
                    rows_out(("KV", 0))
                else:
                    for i in range(1, NQ):
                        g = i // TPB - 1
                        scores(i, 0)
                        scores(i, 1)
                        if U.kind == TURN and i > 1:
                            for n in X_IN_STEP[i - 1][1:]:
                                rows_in(n)
                        if i == 1:
                            scores(i, 2)
                            scores(i, 3)
                            turn(i - 1, 0)
                            turn(i - 1, 1)
                        else:
                            turn(i - 1, 0)
                            scores(i, 2)
                            turn(i - 1, 1)
                            scores(i, 3)
                        if i % 2 == 0:
                            turn(i - 1, 2)
                            turn(i - 1, 3)
                            pv(g, first_half)
                        else:
                            if g >= 0:
                                pv(g, rest[:4])
                            turn(i - 1, 2)
                            if g >= 0:
                                pv(g, rest[4:])
                            turn(i - 1, 3)
                        if U.kind == TURN:
                            for n in X_IN_STEP[i][:1 if i < NQ - 1 else None]:
                                rows_in(n)
                    i = NQ - 1
                    if U.has_next():
                        kv(0, SETS[0][0:2])
                    turn(i, 0)
                    turn(i, 1)
                    if U.has_next():
                        kv(0, SETS[0][2:4])
                    turn(i, 2)
                    turn(i, 3)
                    if U.has_next():
                        kv(1, SETS[1][0:2])
                    pv(GR - 1, first_half + rest)
                    if U.has_next():
                        kv(1, SETS[1][2:4])
                        rows_out(("KV", 0))
                if U.has_next():
                    kv(2, SETS[2])
                    rows_out(("KV", 1))
                    queries(0)
                    kv(3, SETS[3])
                    rows_out(("KV", 2))
                    rows_out(("Q", 0))
                    queries(1)
                    scores(NQ, 0)
                    scores(NQ, 1)
                heads = list(range(GR))
                if U.kind != START:
                    output(0, heads[:2])
                if U.has_next():
                    rows_out(("KV", 3))
                if U.kind != START:
                    output(0, heads[2:])
                if U.has_next():
                    scores(NQ, 2)
                    rows_out(("Q", 1))
                    scores(NQ, 3)
                if U.kind != START:
                    output(1, heads)
                if U.has_next():
                    e.wait_ge(s_free, U.free("QT", 1))
            units(e, body)

        @block.scalar
        def _(e):
            e.preload_act_table_set("natural_log_exp_and_others")
            e.wait_ge(s_pad, 3)

            def body(U):
                u = U.u

                def load_rows(n):
                    rows = P if n < NJ - 1 else TAIL
                    b = 0 if U.kind == START else U.b + 1
                    if n < TPB:
                        src = x1[bass.ds(b, 1), n * P:n * P + rows, :]
                    else:
                        src = ctx_in[bass.ds(b, 1), (n - TPB) * P:(n - TPB) * P + rows, :]
                    if U.kind == START:
                        if n >= FIRST:
                            e.wait_ge(s_full, U.ring("X", n - FIRST))
                    elif n >= 2:
                        e.wait_ge(s_full, U.ring("X", n - 2))
                    else:
                        e.wait_ge(s_full, U.ring0)
                    e.dma_start(key_rows(U.kind, n)[0:rows, :], src.rearrange("o p e -> (o p) e"))\
                        .then_inc(s_xf[n % FIRST] if U.kind == START else s_xd[n % 2], 16)

                def hi(*label):
                    ps, dst, _ = target(label, U.bank(*label))
                    e.wait_ge(s_full, U.ring(*label))
                    if label[0] == "QT":
                        e.activation(dst, ps, ACT.Copy, scale=qkw[:, 2:3]).then_inc(s_hi, 1)
                    else:
                        e.activation(dst, ps, ACT.Copy).then_inc(s_hi, 1)
                    ahead = FIRST if U.kind == START else 2
                    if label[0] == "X" and label[1] + ahead < NJ:
                        load_rows(label[1] + ahead)

                def norm(i):
                    e.wait_ge(s_ri, NQ * u + i + 1)
                    p = prob[:, i % 2, SPLIT:NK]
                    e.activation(p, p, ACT.Copy, scale=rinv[:, i % 2, 1:2]).then_inc(s_pa, 1)

                def exps(i, half):
                    at, to = ((0, 512), (512, NK))[half]
                    if half == 0:
                        e.wait_ge(s_nm, NQ * u + i + 1)
                    if half == 0 and i != 1 and U.kind != START:
                        e.wait_ge(s_full, U.ring("T", i - 2, 3))
                    e.activation(prob[:, i % 2, at:to], S_ps[:, at:to], ACT.Exp, bias=nm[:, i % 2:i % 2 + 1],
                                 accum_out=rsum[:, i % 2, half:half + 1]).then_inc(s_exp, 1)

                def out_hi(g):
                    e.wait_ge(s_of, GR * u + g + 1)
                    e.activation(OT_hi[:, g, :], OT_ps[:, 0:TPB * P], ACT.Copy).then_inc(s_oh, 1)

                def squares(job):
                    no = JOBS.index(job)
                    n = job_no(U, job)
                    if job[0] == "Q":
                        e.wait_ge(s_full, U.ring(*job))
                    else:
                        e.wait_ge(s_kv, 4 * (u + 1) + job[1] + 1)
                    if no >= 2:
                        e.wait_ge(s_full, U.ring(*OUT[JOBS[no - 2]]))
                    src = job_source(U, job)
                    k = src.shape[1]
                    e.activation(nat[:, no % 2, 0:k, :], src, ACT.Square).then_inc(s_sq, 1)
                    if job[0] == "KV" and job[1] > 0:
                        v_hi(job[1])
                    if job == ("Q", 1):
                        hi("KT", 3)
                    e.wait_ge(s_ms, n)
                    e.activation(nrm[:, 2, 0:k], nrm[:, 1, 0:k], ACT.Ln).then_inc(s_ln, 1)
                    e.wait_ge(s_ln, n)
                    e.activation(nrm[:, 3, 0:k], nrm[:, 2, 0:k], ACT.Exp, scale=-0.5).then_inc(s_y0, 1)

                def v_hi(g):
                    e.wait_ge(s_kv, 4 * (u + 1) + g + 1)
                    if g == 0:
                        e.wait_ge(s_nat, job_no(U, ("KV", 0)))
                    if g < 2 and U.kind != START:
                        e.wait_ge(s_of, GR * (u + 1))
                    e.activation(V_hi[:, 4 * g:4 * g + len(SETS[g]), :], v_source(g), ACT.Copy).then_inc(s_vh, 1)

                if U.kind == START:
                    for n in range(FIRST):
                        load_rows(n)
                    for n in range(NJ):
                        hi("X", n)
                    e.wait_ge(s_w, 1)
                    squares(("KV", 0))
                    v_hi(0)
                    squares(("KV", 1))
                    hi("KT", 0)
                else:
                    if U.kind == TURN:
                        load_rows(0)
                        load_rows(1)
                    for i in range(1, NQ):
                        hi("T", i - 1, 0)
                        hi("T", i - 1, 1)
                        if i % 2 == 0:
                            hi("T", i - 1, 2)
                            exps(i, 0)
                            exps(i, 1)
                            hi("T", i - 1, 3)
                        else:
                            exps(i, 0)
                            exps(i, 1)
                            hi("T", i - 1, 2)
                            hi("T", i - 1, 3)
                        if U.kind == TURN:
                            hi("X", X_IN_STEP[i][0])
                        norm(i)
                        if i % 2 and i >= 3:
                            out_hi((i - 3) // 2)
                        if U.kind == TURN:
                            for n in X_IN_STEP[i][1:]:
                                hi("X", n)
                    i = NQ - 1
                    hi("T", i, 0)
                    hi("T", i, 1)
                    if U.has_next():
                        squares(("KV", 0))
                    hi("T", i, 2)
                    hi("T", i, 3)
                    out_hi(GR - 1)
                    if U.has_next():
                        v_hi(0)
                        squares(("KV", 1))
                        hi("KT", 0)
                if U.has_next():
                    squares(("KV", 2))
                    hi("KT", 1)
                    squares(("Q", 0))
                    hi("KT", 2)
                    hi("QT", 0)
                    squares(("KV", 3))
                    squares(("Q", 1))
                    hi("QT", 1)
                    exps(NQ, 0)
                    exps(NQ, 1)
                    norm(NQ)
            units(e, body)

        @block.vector
        def _(e):
            e.wait_ge(s_qkw, 32)
            e.scalar_tensor_tensor(qkw[:, 2:3], qkw[:, 0:1], float(HD) ** -0.5, qkw[:, 1:2],
                                   ALU.mult, ALU.mult).then_inc(s_w, 1)
            e.wait_ge(s_w, 1)
            e.wait_ge(s_pad, 3)

            def body(U):
                u = U.u

                def lo(*label):
                    ps, hi, dst = target(label, U.bank(*label))
                    e.wait_ge(s_hi, U.hi(*label))
                    if label[0] == "QT":
                        e.scalar_tensor_tensor(dst, ps, qkw[:, 2:3], f(hi), ALU.mult, ALU.subtract)\
                            .then_inc(s_free, 1)
                    else:
                        e.tensor_tensor(dst, ps, f(hi), ALU.subtract).then_inc(s_free, 1)

                def chunk_max(i, k):
                    at, to, c = ((0, 1024, 1), (1024, 1536, 2), (1536, NK, 3))[k]
                    e.wait_ge(s_sc, 4 * (NQ * u + i) + c + 1)
                    e.reduce_max(pm[:, i % 2, k:k + 1], S_ps[:, at:to], AX.X).then_inc(s_max, 1)

                def negate(i):
                    e.wait_ge(s_max, 3 * (NQ * u + i + 1))
                    e.tensor_reduce(nm[:, i % 2:i % 2 + 1], pm[:, i % 2, :], AX.X, ALU.max, negate=True)\
                        .then_inc(s_nm, 1)

                def norm_rows(i):
                    e.wait_ge(s_ri, NQ * u + i + 1)
                    p = prob[:, i % 2, 0:SPLIT]
                    e.tensor_scalar(p, p, rinv[:, i % 2, 1:2], None, ALU.mult).then_inc(s_pn, 1)

                def reciprocal(i):
                    e.wait_ge(s_exp, 2 * (NQ * u + i + 1))
                    e.tensor_tensor(rinv[:, i % 2, 0:1], rsum[:, i % 2, 0:1], rsum[:, i % 2, 1:2], ALU.add)\
                        .then_inc(s_rs, 1)
                    e.wait_ge(s_rs, NQ * u + i + 1)
                    e.reciprocal(rinv[:, i % 2, 1:2], rinv[:, i % 2, 0:1]).then_inc(s_ri, 1)

                def out_lo(g):
                    e.wait_ge(s_oh, GR * u + g + 1)
                    e.tensor_tensor(OT_lo[:, g, :], OT_ps[:, 0:TPB * P], f(OT_hi[:, g, :]), ALU.subtract)\
                        .then_inc(s_ol, 1)

                def norm(job):
                    no = JOBS.index(job)
                    n = job_no(U, job)
                    src = job_source(U, job)
                    k = src.shape[1]
                    rows = nat[:, no % 2, 0:k, :]
                    e.wait_ge(s_sq, n)
                    e.reduce_sum(nrm[:, 0, 0:k], rows, AX.X).then_inc(s_ss, 1)
                    e.wait_ge(s_ss, n)
                    e.tensor_scalar(nrm[:, 1, 0:k], nrm[:, 0, 0:k], 1.0 / HD, EPS, ALU.mult, ALU.add)\
                        .then_inc(s_ms, 1)
                    if job[0] == "KV" and job[1] > 0:
                        v_lo(job[1])
                    if job == ("Q", 1):
                        lo("KT", 3)
                    e.wait_ge(s_y0, n)
                    newton_rsqrt(e, nc, nrm[:, 1, 0:k], nrm[:, 3, 0:k], nrm[:, 4, 0:k], nrm[:, 5, 0:k],
                                 (s_nw, 3 * n - 3)).then_inc(s_nw, 1)
                    e.wait_ge(s_nw, 3 * n)
                    e.tensor_tensor(rows, src, nrm[:, 5, 0:k].unsqueeze(2).to_broadcast([P, k, HD]),
                                    ALU.mult).then_inc(s_nat, 1)

                def v_lo(g):
                    e.wait_ge(s_vh, 4 * (u + 1) + g + 1)
                    at = slice(4 * g, 4 * g + len(SETS[g]))
                    e.tensor_tensor(V_lo[:, at, :], v_source(g), f(V_hi[:, at, :]), ALU.subtract)\
                        .then_inc(s_vl, 1)

                def add_output(t):
                    e.wait_ge(s_full, U.ring("O", t))
                    if t == 0:
                        e.wait_ge(s_yd, 32 * U.b + 16)
                    e.tensor_tensor(y[:, t, :], y[:, t, :], ring_ps[U.bank("O", t)][:], ALU.add)\
                        .then_inc(s_free, 1)

                if U.kind == START:
                    for n in range(NJ):
                        lo("X", n)
                    norm(("KV", 0))
                    v_lo(0)
                    norm(("KV", 1))
                    lo("KT", 0)
                else:
                    for i in range(1, NQ):
                        chunk_max(i, 0)
                        if U.kind == TURN and i > 1:
                            for n in X_IN_STEP[i - 1][1:]:
                                lo("X", n)
                        if i % 2 == 0 and U.kind != TURN:
                            lo("T", i - 2, 3)
                            if i >= 4:
                                out_lo((i - 4) // 2)
                        if i % 2 == 0:
                            lo("T", i - 1, 0)
                        chunk_max(i, 1)
                        chunk_max(i, 2)
                        negate(i)
                        if i % 2:
                            lo("T", i - 1, 0)
                        lo("T", i - 1, 1)
                        if i % 2 == 0:
                            lo("T", i - 1, 2)
                        reciprocal(i)
                        norm_rows(i)
                        if i % 2:
                            lo("T", i - 1, 2)
                        if i % 2 == 0 or i == NQ - 1 or U.kind == TURN:
                            lo("T", i - 1, 3)
                        if i % 2 and i >= 3 and (i == NQ - 1 or U.kind == TURN):
                            out_lo((i - 3) // 2)
                        if U.kind == TURN:
                            for n in X_IN_STEP[i][:1 if i < NQ - 1 else None]:
                                lo("X", n)
                    i = NQ - 1
                    lo("T", i, 0)
                    lo("T", i, 1)
                    if U.has_next():
                        norm(("KV", 0))
                    lo("T", i, 2)
                    lo("T", i, 3)
                    out_lo(GR - 1)
                    if U.has_next():
                        v_lo(0)
                        norm(("KV", 1))
                        lo("KT", 0)
                if U.has_next():
                    norm(("KV", 2))
                    lo("KT", 1)
                    norm(("Q", 0))
                    lo("KT", 2)
                    lo("QT", 0)
                    norm(("KV", 3))
                    chunk_max(NQ, 0)
                    norm(("Q", 1))
                    chunk_max(NQ, 1)
                    chunk_max(NQ, 2)
                    negate(NQ)
                    if U.kind != START:
                        add_output(0)
                    lo("QT", 1)
                    if U.kind != START:
                        add_output(1)
                    reciprocal(NQ)
                    norm_rows(NQ)
                else:
                    add_output(0)
                    add_output(1)
            units(e, body)


def feed_forward(nc, y_in, Wr, rb, eb, out):
    B, S, E = y_in.shape
    NE = Wr.shape[0]
    C = E // P
    TOP = 8

    N = B * S // P
    K = 4
    GROUPS = N // K
    assert GROUPS == 2 and K * NE <= 512 and K * P <= 512

    with ExitStack() as ctx:
        def sb(name, shape, dt=F32):
            return ctx.enter_context(nc.sbuf_tensor(name, shape, dt))

        def sem(name):
            return ctx.enter_context(nc.semaphore(name))

        def tiles(g):
            return range(K * g, K * g + K)

        def of(g):
            return slice(K * g, K * g + K)

        y = sb("f_y", [P, N, E])
        z = sb("f_z", [P, N, E])
        xT = sb("f_xT", [P, 2, C, P])
        wr = sb("f_wr", [NE, E])
        wrT = sb("f_wrT", [P, C, NE])
        ebs = sb("f_eb", [NE, E])
        rbs = sb("f_rb", [1, NE])
        ones = sb("f_ones", [1, P])
        ident = sb("f_ident", [P, P])
        bn = sb("f_bn", [P, N, 6])
        mv = sb("f_mv", [P, N, 2])
        rs = sb("f_rs", [P, 5, N])
        soft = sb("f_soft", [P, 4, N])
        ex = sb("f_exp", [P, N, NE])
        rest = sb("f_rest", [P, N, NE])
        top = sb("f_top", [P, N, TOP])
        wT = sb("f_wT", [NE, GROUPS, K, P])
        tr = [ctx.enter_context(nc.psum_tensor(f"f_tr{i}", [P, 512], F32)) for i in range(2)]
        lg = [ctx.enter_context(nc.psum_tensor(f"f_lg{i}", [P, K, NE], F32)) for i in range(2)]
        tw = [ctx.enter_context(nc.psum_tensor(f"f_tw{i}", [P, 512], F32)) for i in range(2)]
        mx = [ctx.enter_context(nc.psum_tensor(f"f_mx{i}", [P, 512], F32)) for i in range(2)]

        s_w = sem("f_weights_loaded")
        s_c = sem("f_constants")
        s_y = [sem(f"f_y_loaded{n}") for n in range(N)]
        s_wt = sem("f_router_transposed")
        s_wc = sem("f_router_copied")
        s_bn = sem("f_bn_stats")
        s_ag = sem("f_bn_aggregates")
        s_va = sem("f_variances")
        s_ln = sem("f_log_variances")
        s_y0 = sem("f_rsqrt_estimates")
        s_nw = sem("f_newton_steps")
        s_x2 = sem("f_x2")
        s_tr = sem("f_x2_transposed")
        s_xT = sem("f_x2T_copied")
        s_lg = sem("f_logits")
        s_mm = sem("f_row_max")
        s_sh = sem("f_logits_shifted")
        s_ex = sem("f_exponentials")
        s_su = sem("f_row_sums")
        s_ri = sem("f_row_reciprocals")
        s_pr = sem("f_probabilities")
        s_tp = sem("f_top_values")
        s_re = sem("f_scores_that_stay")
        s_ts = sem("f_top_sums")
        s_tk = sem("f_top_weights")
        s_tw = sem("f_weights_transposed")
        s_tc = sem("f_weights_copied")
        s_mx = sem("f_mixed")
        s_z = sem("f_z")
        s_ou = sem("f_normed")
        s_st = sem("f_stored")

        block = ctx.enter_context(nc.Block())
        yv = y_in.rearrange("b (t p) e -> p (b t) e", p=P)
        ov = out.rearrange("b (t p) e -> p (b t) e", p=P)

        @block.sync
        def _(e):
            for n in range(N):
                e.dma_start(y[:, n, :], yv[:, n, :]).then_inc(s_y[n], 16)
            for n in range(N):
                e.wait_ge(s_ou, n + 1)
                e.dma_start(ov[:, n, :], z[:, n, :]).then_inc(s_st, 16)
            e.wait_ge(s_st, 16 * N)

        @block.gpsimd
        def _(e):
            e.memset(ones[:], 1.0).then_inc(s_c, 1)
            e.memset(ident[:], 0.0).then_inc(s_c, 1)
            e.wait_ge(s_c, 2)
            e.affine_select(out=ident[:], in_=ident[:], compare_op=ALU.not_equal, fill=1.0, base=0,
                            pattern=[[-1, P]], channel_multiplier=1).then_inc(s_c, 1)

        @block.tensor
        def _(e):
            e.wait_ge(s_c, 3)
            e.wait_ge(s_w, 48)
            for c in range(C):
                ins = e.transpose(tw[0][:, c * NE:(c + 1) * NE], wr[:, c * P:(c + 1) * P], ident[0:NE, 0:NE])
            ins.then_inc(s_wt, 1)
            e.wait_ge(s_wc, 1)

            def turn(n):
                e.wait_ge(s_x2, n + 1)
                if n >= 2:
                    e.wait_ge(s_xT, n - 1)
                for c in range(C):
                    ins = e.transpose(tr[n % 2][:, c * P:(c + 1) * P], y[:, n, c * P:(c + 1) * P], ident[:])
                ins.then_inc(s_tr, 1)

            def logits(n):
                e.wait_ge(s_xT, n + 1)
                out = lg[n // K][:, n % K, :]
                for c in range(C):
                    e.matmul(out, xT[:, n % 2, c, :], wrT[:, c, :], start=(c == 0), stop=False)
                e.matmul(out, ones[:], rbs[:], start=False, stop=True).then_inc(s_lg, 1)

            def mix(g):
                e.wait_ge(s_tk, g + 1)
                for n in tiles(g):
                    ins = e.transpose(tw[g][0:NE, n % K * P:(n % K + 1) * P], rest[:, n, :], ident[:])
                ins.then_inc(s_tw, 1)
                e.wait_ge(s_tc, g + 1)
                for n in tiles(g):
                    if n >= 2:
                        e.wait_ge(s_z, n - 1)
                    e.matmul(mx[n % 2][:], wT[:, g, n % K, :], ebs[:], start=True, stop=True).then_inc(s_mx, 1)

            for n in range(N + 1):
                if n < N:
                    turn(n)
                if n >= 1:
                    logits(n - 1)
            for g in range(GROUPS):
                mix(g)

        @block.scalar
        def _(e):
            e.dma_start(wr[:], Wr).then_inc(s_w, 16)
            e.dma_start(ebs[:], eb).then_inc(s_w, 16)
            e.dma_start(rbs[:], rb.rearrange("(o n) -> o n", o=1)).then_inc(s_w, 16)
            e.preload_act_table_set("natural_log_exp_and_others")
            e.wait_ge(s_wt, 1)
            e.activation(wrT[:], tw[0][:, 0:C * NE].rearrange("p (c n) -> p c n", n=NE), ACT.Copy)\
                .then_inc(s_wc, 1)

            def rsqrt(k, g):
                at = GROUPS * k + g
                e.wait_ge(s_va, at + 1)
                e.activation(rs[:, 1, of(g)], rs[:, 0, of(g)], ACT.Ln).then_inc(s_ln, 1)
                e.wait_ge(s_ln, at + 1)
                e.activation(rs[:, 2, of(g)], rs[:, 1, of(g)], ACT.Exp, scale=-0.5).then_inc(s_y0, 1)

            def exponentials(g):
                e.wait_ge(s_sh, g + 1)
                e.activation(ex[:, of(g), :], ex[:, of(g), :], ACT.Exp).then_inc(s_ex, 1)

            rsqrt(0, 0)
            rsqrt(0, 1)
            for n in range(N):
                e.wait_ge(s_tr, n + 1)
                if n >= 2:
                    e.wait_ge(s_lg, n - 1)
                e.activation(xT[:, n % 2].rearrange("p c k -> p (c k)"), tr[n % 2][:], ACT.Copy)\
                    .then_inc(s_xT, 1)
                if n == K + 1:
                    exponentials(0)
            exponentials(1)
            for g in range(GROUPS):
                e.wait_ge(s_tw, g + 1)
                e.activation(wT[:, g].rearrange("e k p -> e (k p)"), tw[g][0:NE, :], ACT.Copy).then_inc(s_tc, 1)
            rsqrt(1, 0)
            rsqrt(1, 1)

        @block.vector
        def _(e):
            def stats(k, g, src, n):
                e.bn_stats(bn[:, n, :], src[:, n, :]).then_inc(s_bn, 1)

            def variances(k, g):
                e.wait_ge(s_bn, N * k + K * (g + 1))
                for n in tiles(g):
                    e.bn_aggr(mv[:, n, :], bn[:, n, :]).then_inc(s_ag, 1)
                e.wait_ge(s_ag, N * k + K * (g + 1))
                e.tensor_scalar(rs[:, 0, of(g)], mv[:, of(g), 1], 1e-5, None, ALU.add).then_inc(s_va, 1)

            def apply(k, g, src, done):
                at = GROUPS * k + g
                e.wait_ge(s_y0, at + 1)
                newton_rsqrt(e, nc, rs[:, 0, of(g)], rs[:, 2, of(g)], rs[:, 3, of(g)], rs[:, 4, of(g)],
                             (s_nw, 3 * at)).then_inc(s_nw, 1)
                e.wait_ge(s_nw, 3 * at + 3)
                for n in tiles(g):
                    e.tensor_scalar(src[:, n, :], src[:, n, :], mv[:, n, 0:1], rs[:, 4, n:n + 1],
                                    ALU.subtract, ALU.mult).then_inc(done, 1)

            def spread(j, g):
                return soft[:, j, of(g)].unsqueeze(2).to_broadcast([P, K, NE])

            def shift(g):
                e.wait_ge(s_lg, K * (g + 1))
                e.reduce_max(soft[:, 0, of(g)], lg[g][:], AX.X).then_inc(s_mm, 1)
                e.wait_ge(s_mm, g + 1)
                e.tensor_tensor(ex[:, of(g), :], lg[g][:], spread(0, g), ALU.subtract).then_inc(s_sh, 1)

            def weights(g):
                e.wait_ge(s_ex, g + 1)
                e.reduce_sum(soft[:, 1, of(g)], ex[:, of(g), :], AX.X).then_inc(s_su, 1)
                e.wait_ge(s_su, g + 1)
                e.reciprocal(soft[:, 2, of(g)], soft[:, 1, of(g)]).then_inc(s_ri, 1)
                e.wait_ge(s_ri, g + 1)
                e.tensor_tensor(ex[:, of(g), :], ex[:, of(g), :], spread(2, g), ALU.mult).then_inc(s_pr, 1)
                e.wait_ge(s_pr, g + 1)
                for n in tiles(g):
                    e.max(top[:, n, :], ex[:, n, :]).then_inc(s_tp, 1)
                e.wait_ge(s_tp, K * (g + 1))
                for n in tiles(g):
                    e.match_replace(rest[:, n, :], top[:, n, :], ex[:, n, :], 0.0).then_inc(s_re, 1)
                e.reduce_sum(soft[:, 3, of(g)], top[:, of(g), :], AX.X).then_inc(s_ts, 1)
                e.wait_ge(s_re, K * (g + 1))
                e.tensor_tensor(rest[:, of(g), :], ex[:, of(g), :], rest[:, of(g), :], ALU.subtract)\
                    .then_inc(s_tk, 1)
                e.wait_ge(s_ts, 2 * g + 1)
                e.tensor_scalar(soft[:, 3, of(g)], soft[:, 3, of(g)], 1.0, None, ALU.add).then_inc(s_ts, 1)

            def combine(n):
                e.wait_ge(s_mx, n + 1)
                e.wait_ge(s_ts, 2 * (n // K) + 2)
                e.scalar_tensor_tensor(z[:, n, :], y[:, n, :], soft[:, 3, n:n + 1], mx[n % 2][:],
                                       ALU.mult, ALU.add).then_inc(s_z, 1)

            for g in range(GROUPS):
                for n in tiles(g):
                    e.wait_ge(s_y[n], 16)
                    stats(0, g, y, n)
                variances(0, g)
            for g in range(GROUPS):
                apply(0, g, y, s_x2)
            for g in range(GROUPS):
                shift(g)
                weights(g)
            for g in range(GROUPS):
                for n in tiles(g):
                    combine(n)
                    e.wait_ge(s_z, n + 1)
                    stats(1, g, z, n)
                variances(1, g)
                if g:
                    apply(1, g - 1, z, s_ou)
            apply(1, GROUPS - 1, z, s_ou)


def decoder_layer(nc, x, ctx_4096, sWq, sbq, sWk, sbk, sWv, sbv, xWq, xWk, xWv, xWo, xqw, xkw,
                  Wr, rb, eb, out):
    x1 = nc.dram_tensor("x1_scratch", x.shape, F32, kind="Internal").ap()
    x2 = nc.dram_tensor("x2_scratch", x.shape, F32, kind="Internal").ap()
    self_attention(nc, x, sWq, sbq, sWk, sbk, sWv, sbv, x1)
    cross_attention(nc, ctx_4096, xWq, xWk, xWv, xWo, xqw, xkw, x1, x2)
    feed_forward(nc, x2, Wr, rb, eb, out)


_INS = ["x", "ctx_4096", "L0_attn_Wq", "L0_attn_bq", "L0_attn_Wk", "L0_attn_bk", "L0_attn_Wv", "L0_attn_bv",
        "L0_xattn_Wq", "L0_xattn_Wk", "L0_xattn_Wv", "L0_xattn_Wo", "L0_xattn_q_norm_w",
        "L0_xattn_k_norm_w", "L0_ffn_router_weight", "L0_ffn_router_bias", "L0_ffn_expert_bias"]


def kernel(**inputs):
    import numpy as _np
    import concourse.bacc as _bacc
    from concourse import mybir as _mybir
    from concourse.bass_utils import run_bass_kernel_spmd as _run

    nc = _bacc.Bacc("TRN2", target_bir_lowering=False, num_devices=1)
    arrays, args = {}, []
    for name in _INS:
        a = _np.ascontiguousarray(inputs[name])
        arrays[f"in_{name}"] = a
        args.append(nc.dram_tensor(f"in_{name}", a.shape, _mybir.dt.from_np(a.dtype), kind="ExternalInput").ap())
    out = nc.dram_tensor("out_0", inputs["x"].shape, _mybir.dt.float32, kind="ExternalOutput").ap()
    decoder_layer(nc, *args, out)
    r = _run(nc, [arrays], core_ids=[0])
    return r.results[0]["out_0"]
```
